# Optimizing a Trainium2 kernel written in Bass

```python
import numpy as np
import jax
import jax.numpy as jnp

def _softmax(x, axis=-1):
    return jax.nn.softmax(x, axis=axis)

def _gelu(x):
    return jax.nn.gelu(x, approximate=True)

def _silu(x):
    return jax.nn.silu(x)

def _sigmoid(x):
    return jax.nn.sigmoid(x)

def _layernorm(x, axis=-1, eps=1e-05):
    m = jnp.mean(x, axis=axis, keepdims=True)
    v = jnp.var(x, axis=axis, keepdims=True)
    return (x - m) / jnp.sqrt(v + eps)

def _scatter_add(tgt, idx, src, axis=0):
    return tgt.at[idx].add(src)

def _segment_sum(src, seg, n):
    return jax.ops.segment_sum(src, seg, n)
kernel_name = 'mk_prb_d1_jaxref_r8_89347e'

def setup_inputs(seed: int=0):
    np.random.seed(seed)
    _w = jnp.asarray

    def _L0_attn_setup():
        import jax, jax.numpy as jnp
        import numpy as np
        import math
        B, L, H, D, HID = (2, 128, 16, 64, 128)

        def _rope_tables(seq_len, dim):
            inv_freq = 1.0 / 10000.0 ** (jnp.arange(0, dim, 2, dtype=jnp.float32) / dim)
            t = jnp.arange(seq_len, dtype=jnp.float32)
            freqs = jnp.outer(t, inv_freq)
            emb = jnp.concatenate([freqs, freqs], -1)
            return (jnp.cos(emb), jnp.sin(emb))

        def _rotate_half(x):
            x1, x2 = jnp.split(x, 2, axis=-1)
            return jnp.concatenate([-x2, x1], axis=-1)

        def _apply_rope(x, cos, sin):
            return x * cos + _rotate_half(x) * sin

        def _forward(x, w_qkv, w_o, log_p, log_a, w1, b1, w2, b2):
            Bx, Lx, _ = x.shape
            qkv = jnp.dot(x, w_qkv).reshape(Bx, Lx, 3, H, D)
            qkv = jnp.transpose(qkv, (2, 0, 3, 1, 4))
            q, k, v = (qkv[0], qkv[1], qkv[2])
            cos, sin = _rope_tables(Lx, D)
            cos, sin = (cos[None, None], sin[None, None])
            q = _apply_rope(q, cos, sin)
            k = _apply_rope(k, cos, sin)
            scale = 1.0 / math.sqrt(D)
            scores = jnp.einsum('bhid,bhjd->bhij', q, k) * scale
            pos = jnp.arange(Lx, dtype=jnp.float32)
            dist = jnp.abs(pos[None, :] - pos[:, None])
            p = jax.nn.softplus(log_p)
            a = jax.nn.softplus(log_a)
            kerple = -p * jnp.log1p(a * dist[None])
            attn_t = jnp.transpose(scores, (0, 2, 3, 1))
            kerple_t = jnp.broadcast_to(jnp.transpose(kerple, (1, 2, 0))[None], attn_t.shape)
            combined = jnp.concatenate([attn_t, kerple_t], axis=-1)
            hdn = jax.nn.gelu(jnp.dot(combined, w1) + b1, approximate=False)
            refined = jnp.dot(hdn, w2) + b2
            refined = jnp.transpose(refined, (0, 3, 1, 2))
            scores = scores + kerple[None] + refined
            causal = jnp.tril(jnp.ones((Lx, Lx), dtype=bool))
            scores = jnp.where(causal[None, None], scores, -jnp.inf)
            weights = jax.nn.softmax(scores, axis=-1)
            out = jnp.einsum('bhij,bhjd->bhid', weights, v)
            out = jnp.transpose(out, (0, 2, 1, 3)).reshape(Bx, Lx, H * D)
            return jnp.dot(out, w_o)
        key = jax.random.key(seed)
        ks = jax.random.split(key, 8)
        s = 0.02
        return {'x': jax.random.normal(ks[0], (B, L, HID), jnp.float32), 'w_qkv': jax.random.normal(ks[1], (HID, 3 * H * D), jnp.float32) * s, 'w_o': jax.random.normal(ks[2], (H * D, HID), jnp.float32) * s, 'log_p': jax.random.normal(ks[3], (H, 1, 1), jnp.float32) * 0.02, 'log_a': jax.random.normal(ks[4], (H, 1, 1), jnp.float32) * 0.02, 'w1': jax.random.normal(ks[5], (2 * H, 2 * H), jnp.float32) * s, 'b1': jnp.zeros((2 * H,), jnp.float32), 'w2': jax.random.normal(ks[6], (2 * H, H), jnp.float32) * s, 'b2': jnp.zeros((H,), jnp.float32)}
    _L0_attn_in = _L0_attn_setup()

    def _L0_ffn_setup():
        import jax, jax.numpy as jnp
        import numpy as np
        BS, L, D = (4, 256, 128)
        H, E, K = (8, 16, 2)
        HD = D // H
        I = 512 // H
        key = jax.random.key(seed)
        ks = jax.random.split(key, 10)
        s = lambda k, shp, fan: jax.random.normal(k, shp, jnp.float32) / np.sqrt(fan)
        return {'x': jax.random.normal(ks[0], (BS, L, D), jnp.float32), 'Wm': s(ks[1], (D, D), D), 'bm': jnp.zeros((D,), jnp.float32), 'expert_emb': jax.random.normal(ks[2], (HD, E), jnp.float32), 'W1': s(ks[3], (E, HD, I), HD), 'b1': jnp.zeros((E, I), jnp.float32), 'W2': s(ks[4], (E, I, HD), I), 'b2': jnp.zeros((E, HD), jnp.float32), 'Wo': s(ks[5], (D, D), D), 'bo': jnp.zeros((D,), jnp.float32)}
    _L0_ffn_in = _L0_ffn_setup()
    _d = {'L0_attn_x': _L0_attn_in['x'], 'L0_attn_w_qkv': _L0_attn_in['w_qkv'], 'L0_attn_w_o': _L0_attn_in['w_o'], 'L0_attn_log_p': _L0_attn_in['log_p'], 'L0_attn_log_a': _L0_attn_in['log_a'], 'L0_attn_w1': _L0_attn_in['w1'], 'L0_attn_b1': _L0_attn_in['b1'], 'L0_attn_w2': _L0_attn_in['w2'], 'L0_attn_b2': _L0_attn_in['b2'], 'L0_ffn_Wm': _L0_ffn_in['Wm'], 'L0_ffn_bm': _L0_ffn_in['bm'], 'L0_ffn_expert_emb': _L0_ffn_in['expert_emb'], 'L0_ffn_W1': _L0_ffn_in['W1'], 'L0_ffn_b1': _L0_ffn_in['b1'], 'L0_ffn_W2': _L0_ffn_in['W2'], 'L0_ffn_b2': _L0_ffn_in['b2'], 'L0_ffn_Wo': _L0_ffn_in['Wo'], 'L0_ffn_bo': _L0_ffn_in['bo']}
    _x0 = _d['L0_attn_x']
    _d['L0_attn_x'] = jax.random.normal(jax.random.fold_in(jax.random.key(seed), 1), (8, 512, 128), dtype=_x0.dtype)
    del _x0
    return _d

def reference(L0_attn_x, L0_attn_w_qkv, L0_attn_w_o, L0_attn_log_p, L0_attn_log_a, L0_attn_w1, L0_attn_b1, L0_attn_w2, L0_attn_b2, L0_ffn_Wm, L0_ffn_bm, L0_ffn_expert_emb, L0_ffn_W1, L0_ffn_b1, L0_ffn_W2, L0_ffn_b2, L0_ffn_Wo, L0_ffn_bo):

    def _L0_attn_ref(x, w_qkv, w_o, log_p, log_a, w1, b1, w2, b2):
        import jax, jax.numpy as jnp
        import numpy as np
        import math
        B, L, H, D, HID = (2, 128, 16, 64, 128)

        def _rope_tables(seq_len, dim):
            inv_freq = 1.0 / 10000.0 ** (jnp.arange(0, dim, 2, dtype=jnp.float32) / dim)
            t = jnp.arange(seq_len, dtype=jnp.float32)
            freqs = jnp.outer(t, inv_freq)
            emb = jnp.concatenate([freqs, freqs], -1)
            return (jnp.cos(emb), jnp.sin(emb))

        def _rotate_half(x):
            x1, x2 = jnp.split(x, 2, axis=-1)
            return jnp.concatenate([-x2, x1], axis=-1)

        def _apply_rope(x, cos, sin):
            return x * cos + _rotate_half(x) * sin

        def _forward(x, w_qkv, w_o, log_p, log_a, w1, b1, w2, b2):
            Bx, Lx, _ = x.shape
            qkv = jnp.dot(x, w_qkv).reshape(Bx, Lx, 3, H, D)
            qkv = jnp.transpose(qkv, (2, 0, 3, 1, 4))
            q, k, v = (qkv[0], qkv[1], qkv[2])
            cos, sin = _rope_tables(Lx, D)
            cos, sin = (cos[None, None], sin[None, None])
            q = _apply_rope(q, cos, sin)
            k = _apply_rope(k, cos, sin)
            scale = 1.0 / math.sqrt(D)
            scores = jnp.einsum('bhid,bhjd->bhij', q, k) * scale
            pos = jnp.arange(Lx, dtype=jnp.float32)
            dist = jnp.abs(pos[None, :] - pos[:, None])
            p = jax.nn.softplus(log_p)
            a = jax.nn.softplus(log_a)
            kerple = -p * jnp.log1p(a * dist[None])
            attn_t = jnp.transpose(scores, (0, 2, 3, 1))
            kerple_t = jnp.broadcast_to(jnp.transpose(kerple, (1, 2, 0))[None], attn_t.shape)
            combined = jnp.concatenate([attn_t, kerple_t], axis=-1)
            hdn = jax.nn.gelu(jnp.dot(combined, w1) + b1, approximate=False)
            refined = jnp.dot(hdn, w2) + b2
            refined = jnp.transpose(refined, (0, 3, 1, 2))
            scores = scores + kerple[None] + refined
            causal = jnp.tril(jnp.ones((Lx, Lx), dtype=bool))
            scores = jnp.where(causal[None, None], scores, -jnp.inf)
            weights = jax.nn.softmax(scores, axis=-1)
            out = jnp.einsum('bhij,bhjd->bhid', weights, v)
            out = jnp.transpose(out, (0, 2, 1, 3)).reshape(Bx, Lx, H * D)
            return jnp.dot(out, w_o)
        return _forward(x, w_qkv, w_o, log_p, log_a, w1, b1, w2, b2)

    def _L0_ffn_ref(x, Wm, bm, expert_emb, W1, b1, W2, b2, Wo, bo):
        import jax, jax.numpy as jnp
        import numpy as np
        BS, L, D = (4, 256, 128)
        H, E, K = (8, 16, 2)
        HD = D // H
        I = 512 // H
        bs, L_, d = x.shape
        h = x @ Wm + bm
        t = h.reshape(bs * L_ * H, HD)
        logits = t @ expert_emb
        w = jax.nn.softmax(logits, axis=-1)
        topw, topi = jax.lax.top_k(w, K)
        hmid = jax.nn.gelu(jnp.einsum('td,edi->tei', t, W1) + b1, approximate=False)
        eo = jnp.einsum('tei,eio->teo', hmid, W2) + b2
        sel = jnp.take_along_axis(eo, topi[:, :, None], axis=1)
        comb = (sel * topw[:, :, None]).sum(axis=1)
        out = comb.reshape(bs, L_, d)
        return out @ Wo + bo
    x = L0_attn_x
    xn = _layernorm(x, axis=-1)
    x = x + _L0_attn_ref(xn, L0_attn_w_qkv, L0_attn_w_o, L0_attn_log_p, L0_attn_log_a, L0_attn_w1, L0_attn_b1, L0_attn_w2, L0_attn_b2) + _L0_ffn_ref(xn, L0_ffn_Wm, L0_ffn_bm, L0_ffn_expert_emb, L0_ffn_W1, L0_ffn_b1, L0_ffn_W2, L0_ffn_b2, L0_ffn_Wo, L0_ffn_bo)
    return x

_drawn_inputs = setup_inputs


def setup_inputs(seed=0):
    import zlib

    import numpy as np

    out = dict(_drawn_inputs(seed))
    spreads = {'L0_attn_b1': (0.0, 0.8),
     'L0_attn_b2': (0.0, 2.0),
     'L0_ffn_bm': (0.0, 0.1),
     'L0_ffn_b1': (0.0, 0.1),
     'L0_ffn_b2': (0.0, 0.1),
     'L0_ffn_bo': (0.0, 0.1)}
    factors = {'L0_attn_w_qkv': 3.017,
     'L0_attn_w_o': 3.035,
     'L0_attn_log_p': 8.0,
     'L0_attn_log_a': 58.988,
     'L0_attn_w1': 8.0,
     'L0_attn_w2': 8.0}
    for name, (base, spread) in spreads.items():
        noise = np.random.default_rng([zlib.crc32(name.encode()), seed]).standard_normal(out[name].shape)
        drawn = base * np.exp(spread * noise) if base else spread * noise
        out[name] = jnp.asarray(drawn.astype(out[name].dtype))
    for name, factor in factors.items():
        out[name] = (out[name] * factor).astype(out[name].dtype)
    return out
```

```python
from contextlib import ExitStack

import numpy as np

import concourse.bass as bass
from concourse import mybir

F32 = mybir.dt.float32
F32R = mybir.dt.float32r
ALU = mybir.AluOpType
ACT = mybir.ActivationFunctionType
AX = mybir.AxisListType.X

P = 128
B, L, D = 8, 512, 128
ROWS = B * L
BLOCKS = ROWS // P
H, HD = 16, 64
C = 2 * H
PAIRS = H // 2
QB = L // P
TQ = 8
TILES = P // TQ
HALF = TQ // 2
RING = 4
S, SD = 8, 16
E, I = 16, 64
EP = E // 2
CH = 512
CHUNKS = ROWS // CH
EPS = 1e-5
MASKED = -1e30


def shape_constants():
    f = np.float32
    inv_freq = (f(1.0) / np.power(f(10000.0), np.arange(0, HD, 2, dtype=f) / f(HD))).astype(f)
    freqs = np.outer(np.arange(L, dtype=f), inv_freq).astype(f)
    emb = np.concatenate([freqs, freqs], -1)
    cos, sin = np.cos(emb).astype(f).T, np.sin(emb).astype(f).T
    sign = np.where(np.arange(HD) < HD // 2, f(-1), f(1))[:, None]
    cols = np.arange(L) - (L - TQ)
    dist = (np.arange(P) // H)[:, None] - cols[None]
    e_rev = np.broadcast_to((E - np.arange(E)).astype(f), (P, BLOCKS * S, E))
    k = np.arange(P)
    sel = np.zeros((P, S, 2, P), f)
    for s in range(S):
        for half in range(2):
            want = s * E + half * (E // 2) + k // SD
            sel[want, s, half, k] = 1
    return {
        "c_ident": np.eye(P, dtype=f),
        "c_cos": np.concatenate([cos, cos]),
        "c_sin": np.concatenate([sin * sign, sin * sign]),
        "c_dist": np.abs(dist).astype(f),
        "c_mask": np.where(dist < 0, f(MASKED), f(0)),
        "c_erev": np.ascontiguousarray(e_rev[:, 0]),
        "c_sel": sel.reshape(P, S * 2 * P),
    }


def norm_and_gates(nc, x, Wm, bm, emb, c, xnT_dram, gT_dram):
    with ExitStack() as ctx:
        def sb(name, shape, dt=F32):
            return ctx.enter_context(nc.sbuf_tensor(name, shape, dt))

        def ps(name, shape):
            return ctx.enter_context(nc.psum_tensor(name, shape, F32))

        def sem(name):
            return ctx.enter_context(nc.semaphore(name))

        G = BLOCKS * S
        x_all = sb("x_all", [P, BLOCKS, D])
        ident = sb("n_ident", [P, P])
        wm = sb("n_wm", [D, D])
        bmc = sb("n_bmc", [D, 1])
        emb_bd = sb("emb_bd", [P, P])
        erev = sb("erev", [P, E])
        stats = sb("stats", [P, BLOCKS, 6])
        small = sb("n_small", [P, 5, BLOCKS])
        xn = sb("xn", [P, 4, P])
        xT = sb("n_xT", [P, CH])
        hT = sb("n_hT", [P, CH])
        logit = sb("logit", [P, G, E])
        ex = sb("ex", [P, G, E])
        t1 = sb("t1", [P, G, E])
        first = sb("first", [P, G, E])
        red = sb("red", [P, 6, G])
        gT = sb("n_gT", [P, CH])
        pT = ps("n_pT", [P, CH])
        pH = ps("n_pH", [P, CH])
        pL = ps("n_pL", [P, CH])
        pG = ps("n_pG", [P, CH])

        zeroed = sem("n_zeroed")
        consts = sem("n_consts")
        x_loaded = sem("x_loaded")
        step = sem("n_step")
        var_ready = sem("var_ready")
        std_ready = sem("std_ready")
        xn_ready = sem("xn_ready")
        xT_psum = sem("xT_psum")
        xT_ready = sem("xT_ready")
        xT_stored = sem("xT_stored")
        hT_psum = sem("hT_psum")
        hT_ready = sem("hT_ready")
        lg_psum = sem("lg_psum")
        lg_ready = sem("lg_ready")
        diff_ready = sem("diff_ready")
        ex_ready = sem("ex_ready")
        gates_ready = sem("gates_ready")
        gT_psum = sem("gT_psum")
        gT_ready = sem("gT_ready")
        gT_stored = sem("gT_stored")

        N_CONST = 4 + S
        bc = lambda a: a.unsqueeze(2).broadcast_to([P, G, E])

        block = ctx.enter_context(nc.Block())

        @block.sync
        def _(sp):
            sp.sem_inc(xT_stored, 16)
            sp.sem_inc(gT_stored, 16)
            sp.dma_start(x_all[:], x.rearrange("(k p) n -> p k n", p=P)).then_inc(x_loaded, 16)
            sp.dma_start(ident[:], c["c_ident"]).then_inc(consts, 16)
            sp.dma_start(wm[:], Wm).then_inc(consts, 16)
            sp.dma_start(bmc[:], bm.rearrange("(n a) -> n a", a=1)).then_inc(consts, 16)
            sp.dma_start(erev[:], c["c_erev"]).then_inc(consts, 16)
            sp.wait_ge(zeroed, 1)
            for s in range(S):
                sp.dma_start(emb_bd[s * SD:(s + 1) * SD, s * E:(s + 1) * E], emb).then_inc(consts, 16)
            with sp.Fori(0, CHUNKS) as i:
                sp.wait_ge(xT_ready, i + 2)
                sp.dma_start(xnT_dram[i], xT[:]).then_inc(xT_stored, 16)
            with sp.Fori(0, CHUNKS) as i:
                sp.wait_ge(gT_ready, i + 1)
                sp.dma_start(gT_dram[i], gT[:]).then_inc(gT_stored, 16)
            sp.wait_ge(xT_stored, 16 * CHUNKS + 16)
            sp.wait_ge(gT_stored, 16 * CHUNKS + 16)

        @block.gpsimd
        def _(pool):
            nc.gpsimd.memset(emb_bd[:], 0.0).then_inc(zeroed, 1)

        @block.vector
        def _(dve):
            done = [0]

            def link(ins):
                done[0] += 1
                ins.then_inc(step, 1)
                dve.wait_ge(step, done[0])

            dve.sem_inc(lg_ready, 1)
            dve.wait_ge(x_loaded, 16)
            with dve.Fori(0, BLOCKS - 1) as k:
                nc.vector.bn_stats(stats[:, k, :], x_all[:, k, :])
            link(nc.vector.bn_stats(stats[:, BLOCKS - 1, :], x_all[:, BLOCKS - 1, :]))
            mean, var, dm, rstd, nmr = (small[:, j, :] for j in range(5))
            link(nc.vector.tensor_tensor(mean, stats[:, :, 1], stats[:, :, 4], ALU.add))
            link(nc.vector.tensor_tensor(dm, stats[:, :, 1], stats[:, :, 4], ALU.subtract))
            link(nc.vector.tensor_tensor(dm, dm, dm, ALU.mult))
            link(nc.vector.tensor_tensor(var, stats[:, :, 2], stats[:, :, 5], ALU.add))
            link(nc.vector.tensor_scalar(var, var, 1.0 / D, EPS, ALU.mult, ALU.add))
            nc.vector.scalar_tensor_tensor(out=var, in0=dm, scalar=0.25, in1=var, op0=ALU.mult,
                                           op1=ALU.add).then_inc(var_ready, 1)
            dve.wait_ge(std_ready, 1)
            link(nc.vector.reciprocal(rstd, rstd))
            link(nc.vector.scalar_tensor_tensor(out=nmr, in0=mean, scalar=-0.5, in1=rstd, op0=ALU.mult,
                                                op1=ALU.mult))
            with dve.Fori(0, CHUNKS) as i:
                dve.wait_ge(xT_psum, i + 1)
                for j in range(4):
                    last = nc.vector.tensor_scalar(xn[:, j, :], x_all[:, i * 4 + j, :],
                                                   small[:, 3, bass.ds(i * 4 + j, 1)],
                                                   small[:, 4, bass.ds(i * 4 + j, 1)], ALU.mult, ALU.add)
                last.then_inc(xn_ready, 1)
                dve.wait_ge(lg_psum, i + 2)
                nc.vector.tensor_copy(logit[:, bass.ds(i * (4 * S), 4 * S), :],
                                      pL[:].rearrange("p (g e) -> p g e", e=E)).then_inc(lg_ready, 1)
            dve.wait_ge(lg_ready, CHUNKS + 1)
            rmax, ridx, rmax2, ridx2, rsum, rinv = (red[:, j, :] for j in range(6))
            erev_b = erev[:].unsqueeze(1).broadcast_to([P, G, E])
            link(nc.vector.tensor_reduce(rmax, logit[:], AX, ALU.max))
            nc.vector.tensor_tensor(logit[:], logit[:], bc(rmax), ALU.subtract).then_inc(diff_ready, 1)
            dve.wait_ge(diff_ready, 1)
            link(nc.vector.scalar_tensor_tensor(out=t1[:], in0=logit[:], scalar=0.0, in1=erev_b,
                                                op0=ALU.is_equal, op1=ALU.mult))
            link(nc.vector.tensor_reduce(ridx, t1[:], AX, ALU.max))
            link(nc.vector.tensor_tensor(first[:], t1[:], bc(ridx), ALU.is_equal))
            dve.wait_ge(ex_ready, 1)
            link(nc.vector.scalar_tensor_tensor(out=logit[:], in0=first[:], scalar=MASKED, in1=logit[:],
                                                op0=ALU.mult, op1=ALU.add))
            link(nc.vector.tensor_reduce(rmax2, logit[:], AX, ALU.max))
            link(nc.vector.tensor_tensor(t1[:], logit[:], bc(rmax2), ALU.is_equal))
            link(nc.vector.tensor_tensor(t1[:], t1[:], erev_b, ALU.mult))
            link(nc.vector.tensor_reduce(ridx2, t1[:], AX, ALU.max))
            link(nc.vector.tensor_tensor(t1[:], t1[:], bc(ridx2), ALU.is_equal))
            link(nc.vector.tensor_tensor(first[:], first[:], t1[:], ALU.add))
            link(nc.vector.tensor_reduce(rsum, ex[:], AX, ALU.add))
            link(nc.vector.reciprocal(rinv, rsum))
            link(nc.vector.tensor_tensor(ex[:], ex[:], first[:], ALU.mult))
            nc.vector.tensor_tensor(ex[:], ex[:], bc(rinv), ALU.mult).then_inc(gates_ready, 1)

        @block.scalar
        def _(act):
            act.sem_inc(xT_ready, 1)
            act.sem_inc(hT_ready, 1)
            act.wait_ge(var_ready, 1)
            nc.scalar.activation(small[:, 3, :], small[:, 1, :], ACT.Sqrt).then_inc(std_ready, 1)
            act.wait_ge(consts, 16 * N_CONST)
            with act.Fori(0, CHUNKS) as i:
                act.wait_ge(xT_stored, i * 16 + 16)
                act.wait_ge(xT_psum, i + 2)
                nc.scalar.activation(xT[:], pT[:], ACT.Copy).then_inc(xT_ready, 1)
                act.wait_ge(lg_psum, i + 1)
                act.wait_ge(hT_psum, i + 1)
                nc.scalar.activation(hT[:], pH[:], ACT.Identity, bias=bmc[:]).then_inc(hT_ready, 1)
            act.wait_ge(diff_ready, 1)
            nc.scalar.activation(ex[:], logit[:], ACT.Exp).then_inc(ex_ready, 1)
            with act.Fori(0, CHUNKS) as i:
                act.wait_ge(gT_stored, i * 16 + 16)
                act.wait_ge(gT_psum, i + 1)
                nc.scalar.activation(gT[:], pG[:], ACT.Copy).then_inc(gT_ready, 1)

        @block.tensor
        def _(pe):
            pe.sem_inc(xT_psum, 1)
            pe.sem_inc(lg_psum, 1)
            pe.wait_ge(consts, 16 * N_CONST)
            with pe.Fori(0, CHUNKS) as i:
                pe.wait_ge(xT_ready, i + 1)
                pe.wait_ge(xn_ready, i + 1)
                for j in range(4):
                    last = nc.tensor.transpose(pT[:, j * P:(j + 1) * P], xn[:, j, :], ident[:])
                last.then_inc(xT_psum, 1)
                pe.wait_ge(hT_ready, i + 1)
                pe.wait_ge(xT_ready, i + 2)
                nc.tensor.matmul(pH[:], wm[:], xT[:], start=True, stop=True).then_inc(hT_psum, 1)
                pe.wait_ge(lg_ready, i + 1)
                pe.wait_ge(hT_ready, i + 2)
                for j in range(4):
                    last = nc.tensor.matmul(pL[:, j * P:(j + 1) * P], hT[:, j * P:(j + 1) * P], emb_bd[:],
                                            start=True, stop=True)
                last.then_inc(lg_psum, 1)
            pe.wait_ge(gates_ready, 1)
            for i in range(CHUNKS):
                if i:
                    pe.wait_ge(gT_ready, i)
                for j in range(4):
                    k = 4 * i + j
                    last = nc.tensor.transpose(pG[:, j * P:(j + 1) * P],
                                               ex[:, k * S:(k + 1) * S, :].rearrange("p g e -> p (g e)"), ident[:])
                last.then_inc(gT_psum, 1)


def experts(nc, x, Wm, bm, W1, b1, W2, b2, Wo, bo, c, xnT_dram, gT_dram, xf_dram):
    with ExitStack() as ctx:
        def sb(name, shape, dt=F32):
            return ctx.enter_context(nc.sbuf_tensor(name, shape, dt))

        def ps(name, shape):
            return ctx.enter_context(nc.psum_tensor(name, shape, F32))

        def sem(name):
            return ctx.enter_context(nc.semaphore(name))

        PARTS = 4
        SP = S // 2
        Q = 2 * SD
        UNITS = 2 * S
        EU = EP // 2
        HB, AB = 2, 4

        ident = sb("e_ident", [P, P])
        wm_rep = sb("wm_rep", [D, SP, PARTS, Q])
        bm_rep = sb("bm_rep", [P, SP])
        w1f = sb("w1f", [P, 2, E * I])
        w1r = sb("w1r", [P, 2, EP, 2 * I], F32R)
        b1c = sb("b1c", [P, EP])
        w2p = sb("w2p", [P, EP, 2 * SD])
        b2c = sb("b2c", [P, 2])
        wo_rep = sb("wo_rep", [P, S, D])
        boc = sb("boc", [P, 1])
        self_ = sb("self", [P, UNITS, P])
        selr = sb("selr", [P, UNITS, P], F32R)
        xT = sb("e_xT", [P, CH])
        gT = sb("e_gT", [P, CH])
        xr = sb("e_xr", [P, CH // P, D])
        tt = sb("tt", [P, CH])
        tr = sb("tr", [P, 2, SP, CH], F32R)
        g_hi = sb("g_hi", [P, 2, CH], F32R)
        g_lo = sb("g_lo", [P, 2, CH], F32R)
        hid = sb("e_hid", [P, AB, CH])
        gs = sb("gs", [P, 2, CH])
        z = sb("z", [P, 2, CH])
        yT = sb("yT", [P, CH])
        xf = sb("xf", [P, CH // P, D])

        p_hid = ps("e_phid", [P, HB, CH])
        p_eo = ps("p_eo", [P, 2, CH])
        p_g = ps("p_g", [P, 2, CH])
        p_y = ps("p_y", [P, CH])
        p_m = ps("p_m", [P, CH])

        zeroed = sem("e_zeroed")
        consts = sem("e_consts")
        w1_hi = sem("w1_hi")
        weights = sem("weights")
        xT_loaded = sem("e_xT_loaded")
        gT_loaded = sem("gT_loaded")
        xr_loaded = sem("e_xr_loaded")
        t_psum = sem("t_psum")
        t_ready = sem("t_ready")
        tr_hi = sem("tr_hi")
        tr_ready = sem("tr_ready")
        g_hi_ready = sem("g_hi_ready")
        g_split = sem("g_split")
        up_done = sem("up_done")
        gelu_done = sem("e_gelu_done")
        down_done = sem("down_done")
        g_psum = sem("g_psum")
        g_ready = sem("g_ready")
        z_ready = sem("z_ready")
        wo_done = sem("wo_done")
        yT_ready = sem("yT_ready")
        y_psum = sem("y_psum")
        xf_ready = sem("xf_ready")
        xf_stored = sem("xf_stored")

        N_CONST = 1 + PARTS + PARTS + 2 * PARTS + 2 + 2 + 1 + E // 2 + 1 + 1

        def over_chunks(eng, chunk):
            with eng.Fori(0, CHUNKS // 2 - 1) as i:
                chunk(2 * i, 0, False)
                chunk(2 * i + 1, 1, False)
            chunk(CHUNKS - 2, 0, False)
            chunk(CHUNKS - 1, 1, True)

        block = ctx.enter_context(nc.Block())

        @block.sync
        def _(sp):
            sp.sem_inc(xf_stored, 16)
            sp.dma_start(xT[:], xnT_dram[0]).then_inc(xT_loaded, 16)
            sp.dma_start(gT[:], gT_dram[0]).then_inc(gT_loaded, 16)
            sp.dma_start(ident[:], c["c_ident"]).then_inc(consts, 16)
            for part in range(PARTS):
                sp.dma_start(wm_rep[:, :, part, :], Wm.rearrange("k (s q) -> k s q", q=Q)).then_inc(consts, 16)
                sp.dma_start(bm_rep[part * Q:(part + 1) * Q, :], bm.rearrange("(s q) -> q s", q=Q),
                             allow_slow_non_contiguous=True)\
                    .then_inc(consts, 16)
            sp.wait_ge(zeroed, 1)
            for part in range(PARTS):
                for s in range(2):
                    r = part * Q + s * SD
                    sp.dma_start(w1f[r:r + SD, s, :].rearrange("d (e i) -> d e i", i=I),
                                 W1.rearrange("e d i -> d e i")).then_inc(consts, 16)
            sp.wait_ge(zeroed, 2)
            w2v = W2.rearrange("(ep two) i o -> two i ep o", two=2)
            b1v = b1.rearrange("(ep two) i -> two i ep", two=2)
            for e in range(2):
                sp.dma_start(w2p[e * I:(e + 1) * I, :, e * SD:(e + 1) * SD], w2v[e]).then_inc(consts, 16)
                sp.dma_start(b1c[e * I:(e + 1) * I, :], b1v[e], allow_slow_non_contiguous=True).then_inc(consts, 16)
            sp.dma_start(b2c[:], b2.rearrange("(h e) o -> (e o) h", h=2), allow_slow_non_contiguous=True).then_inc(consts, 16)
            for e in range(E // 2):
                sp.dma_start(wo_rep[e * SD:(e + 1) * SD, :, :], Wo.rearrange("(s o) n -> o s n", o=SD))\
                    .then_inc(consts, 16)
            sp.dma_start(boc[:], bo.rearrange("(n a) -> n a", a=1)).then_inc(consts, 16)
            sp.dma_start(self_[:], c["c_sel"].rearrange("p (u k) -> p u k", k=P)).then_inc(consts, 16)

            def chunk(n, par, last):
                if not last:
                    sp.wait_ge(t_psum, 4 * n + 4)
                    sp.dma_start(xT[:], xnT_dram[n + 1]).then_inc(xT_loaded, 16)
                    sp.wait_ge(g_split, n + 1)
                    sp.dma_start(gT[:], gT_dram[n + 1]).then_inc(gT_loaded, 16)
                sp.wait_ge(xf_ready, n + 1)
                sp.dma_start(xr[:], x.rearrange("(c k p) n -> c p k n", k=CH // P, p=P)[n]).then_inc(xr_loaded, 16)
                sp.wait_ge(xf_ready, n + 2)
                sp.dma_start(xf_dram.rearrange("(c k p) n -> c p k n", k=CH // P, p=P)[n], xf[:])\
                    .then_inc(xf_stored, 16)

            over_chunks(sp, chunk)
            sp.wait_ge(xf_stored, 16 * CHUNKS + 16)

        @block.gpsimd
        def _(pool):
            nc.gpsimd.memset(w1f[:], 0.0).then_inc(zeroed, 1)
            nc.gpsimd.memset(w2p[:], 0.0).then_inc(zeroed, 1)
            pool.wait_ge(consts, 16 * N_CONST)
            nc.gpsimd.tensor_copy(selr[:], self_[:]).then_inc(weights, 1)

        @block.scalar
        def _(act):
            act.sem_inc(gelu_done, HB)
            act.wait_ge(consts, 16 * N_CONST)

            def slots(n, k):
                act.wait_ge(tr_ready, 4 * n + k + 1)
                act.wait_ge(t_psum, 4 * n + k + 1)
                nc.scalar.activation(tt[:], p_m[:], ACT.Identity, bias=bm_rep[:, k:k + 1]).then_inc(t_ready, 1)

            for k in range(SP):
                slots(0, k)

            def chunk(n, par, last):
                for u in range(UNITS):
                    for q in range(EU):
                        j = EU * u + q
                        k = 64 * n + j
                        act.wait_ge(up_done, k + 1)
                        act.wait_ge(down_done, k + 1)
                        ep = (u % 2) * EU + q
                        nc.scalar.activation(hid[:, j % AB, :], p_hid[:, j % HB, :], ACT.Gelu,
                                             bias=b1c[:, ep:ep + 1]).then_inc(gelu_done, 1)
                    if not last and u % 2 == 0 and 2 <= u <= 8:
                        slots(n + 1, u // 2 - 1)

            over_chunks(act, chunk)

        @block.vector
        def _(dve):
            dve.sem_inc(tr_ready, 1)
            dve.sem_inc(g_ready, 2)
            dve.sem_inc(z_ready, 2)
            dve.sem_inc(yT_ready, 1)
            dve.sem_inc(xf_ready, 1)
            dve.wait_ge(consts, 16 * N_CONST)
            nc.vector.tensor_copy(w1r[:].rearrange("p s e i -> p s (e i)"), w1f[:]).then_inc(w1_hi, 1)
            dve.wait_ge(w1_hi, 1)
            for part in (1, 3):
                r = slice(part * Q, (part + 1) * Q)
                w = w1r[r].rearrange("p s e i -> p s (e i)")
                nc.vector.tensor_tensor(w, w1f[r], w.bitcast(F32), ALU.subtract).then_inc(weights, 1)

            def split_slots(n, par, k):
                if not isinstance(n, int) or n:
                    dve.wait_ge(up_done, 64 * n - 63)
                dve.wait_ge(t_ready, 4 * n + k + 1)
                nc.vector.tensor_copy(tr[:, par, k, :], tt[:]).then_inc(tr_hi, 1)
                dve.wait_ge(tr_hi, 4 * n + k + 1)
                low = tr[P // 2:, par, k, :]
                nc.vector.tensor_tensor(low, tt[P // 2:, :], low.bitcast(F32), ALU.subtract).then_inc(tr_ready, 1)

            def split_gates(n, par):
                if not isinstance(n, int) or n:
                    dve.wait_ge(g_psum, 16 * n - 15)
                dve.wait_ge(gT_loaded, 16 * n + 16)
                nc.vector.tensor_copy(g_hi[:, par, :], gT[:]).then_inc(g_hi_ready, 1)
                dve.wait_ge(g_hi_ready, n + 1)
                nc.vector.tensor_tensor(g_lo[:, par, :], gT[:], g_hi[:, par, :].bitcast(F32), ALU.subtract)\
                    .then_inc(g_split, 1)

            for k in range(SP):
                split_slots(0, 0, k)
            split_gates(0, 0)

            def chunk(n, par, last):
                for u in range(UNITS):
                    g = 16 * n + u
                    dve.wait_ge(g_psum, g + 1)
                    nc.vector.tensor_copy(gs[:, u % 2, :], p_g[:, u % 2, :]).then_inc(g_ready, 1)
                    dve.wait_ge(wo_done, g + 1)
                    dve.wait_ge(down_done, 4 * g + 4 + AB)
                    dve.wait_ge(g_ready, g + 1 + 2)
                    nc.vector.scalar_tensor_tensor(out=z[:, u % 2, :], in0=p_eo[:, u % 2, :],
                                                   scalar=b2c[:, u % 2:u % 2 + 1], in1=gs[:, u % 2, :],
                                                   op0=ALU.add, op1=ALU.mult).then_inc(z_ready, 1)
                    if not last and u % 2 == 0 and 2 <= u <= 8:
                        split_slots(n + 1, 1 - par, u // 2 - 1)
                    if not last and u == 10:
                        split_gates(n + 1, 1 - par)
                dve.wait_ge(wo_done, 16 * n + 16 + 2)
                dve.wait_ge(y_psum, n + 1)
                nc.vector.tensor_scalar(yT[:], p_y[:], boc[:], None, ALU.add).then_inc(yT_ready, 1)
                dve.wait_ge(xf_stored, 16 * n + 16)
                dve.wait_ge(xr_loaded, 16 * n + 16)
                dve.wait_ge(y_psum, n + 2)
                nc.vector.tensor_tensor(xf[:], p_m[:].rearrange("p (k n) -> p k n", n=D), xr[:], ALU.add)\
                    .then_inc(xf_ready, 1)

            over_chunks(dve, chunk)

        @block.tensor
        def _(pe):
            pe.sem_inc(down_done, AB)
            pe.sem_inc(wo_done, 2)
            pe.sem_inc(y_psum, 1)
            pe.wait_ge(consts, 16 * N_CONST)
            pe.wait_ge(weights, 3)

            def slots(n, k):
                if k:
                    pe.wait_ge(t_ready, 4 * n + k)
                elif not isinstance(n, int) or n:
                    pe.wait_ge(xf_ready, n)
                pe.wait_ge(xT_loaded, 16 * n + 16)
                nc.tensor.matmul(p_m[:], wm_rep[:, k].rearrange("p a q -> p (a q)"), xT[:],
                                 start=True, stop=True).then_inc(t_psum, 1)

            for k in range(SP):
                slots(0, k)

            def chunk(n, par, last):
                pe.wait_ge(g_split, n + 1)
                pe.wait_ge(tr_ready, 4 * n + 4 + 1)

                def down(j):
                    u, q = divmod(j, EU)
                    if q == 0:
                        pe.wait_ge(z_ready, 16 * n + u + 1)
                    pe.wait_ge(gelu_done, 64 * n + j + 1 + HB)
                    nc.tensor.matmul(p_eo[q * 2 * SD:(q + 1) * 2 * SD, u % 2, :], w2p[:, (u % 2) * EU + q, :],
                                     hid[:, j % AB, :], start=True, stop=True).then_inc(down_done, 1)

                def project(u):
                    if u == 0:
                        pe.wait_ge(yT_ready, n + 1)
                    pe.wait_ge(z_ready, 16 * n + u + 1 + 2)
                    nc.tensor.matmul(p_y[:], wo_rep[:, u // 2, :], z[:, u % 2, :],
                                     start=(u == 0), stop=(u == UNITS - 1)).then_inc(wo_done, 1)

                for u in range(UNITS):
                    s = u // 2
                    for q in range(EU):
                        j = EU * u + q
                        pe.wait_ge(gelu_done, 64 * n + j + 1)
                        nc.tensor.matmul(p_hid[:, j % HB, :], w1r[:, s % 2, (u % 2) * EU + q, :],
                                         tr[:, par, s // 2, :], start=True, stop=True).then_inc(up_done, 1)
                        if j >= 2:
                            down(j - 2)
                        if q == 1:
                            pe.wait_ge(g_ready, 16 * n + u + 1)
                            nc.tensor.matmul(p_g[:, u % 2, :], selr[:, u, :], g_hi[:, par, :], start=True, stop=False)
                            nc.tensor.matmul(p_g[:, u % 2, :], selr[:, u, :], g_lo[:, par, :], start=False, stop=True)\
                                .then_inc(g_psum, 1)
                        if q == 3 and u:
                            project(u - 1)
                    if not last and u % 2 == 0 and 2 <= u <= 8:
                        slots(n + 1, u // 2 - 1)
                down(EU * UNITS - 2)
                down(EU * UNITS - 1)
                project(UNITS - 1)
                if not last:
                    pe.wait_ge(t_ready, 4 * n + 8)
                pe.wait_ge(yT_ready, n + 2)
                for k in range(CH // P):
                    last_t = nc.tensor.transpose(p_m[:, k * P:(k + 1) * P], yT[:, k * P:(k + 1) * P], ident[:])
                last_t.then_inc(y_psum, 1)

            over_chunks(pe, chunk)


def attention(nc, w_qkv, w_o, log_p, log_a, w1, b1, w2, b2, c, xnT_dram, xf_dram, out):
    with ExitStack() as ctx:
        def sb(name, shape, dt=F32):
            return ctx.enter_context(nc.sbuf_tensor(name, shape, dt))

        def ps(name, shape):
            return ctx.enter_context(nc.psum_tensor(name, shape, F32))

        def sem(name):
            return ctx.enter_context(nc.semaphore(name))

        HC = HALF * C
        HH = HALF * H

        ident = sb("a_ident", [P, P])
        wqkv = sb("wqkv", [D, 3 * H * HD])
        wo = sb("wo", [P, PAIRS, D])
        w_up = sb("w_up", [P, 2, HC])
        w_down = sb("w_down", [HC, HH])
        cols = sb("cols", [P, 12])
        cos = sb("cos", [P, L])
        sin = sb("sin", [P, L])
        ker_mask = sb("ker_mask", [P, L])
        xa = sb("xa", [P, 2, RING, L])
        sc = sb("sc", [P, RING, L])
        std = sb("std", [P, H, L])
        hid = sb("hid", [P, 2, 2, L])
        pr = sb("pr", [P, TILES, L])
        pT = sb("pT", [P, QB, H, P])
        vv = sb("vv", [P, QB, H * HD])
        kk = sb("kk", [P, PAIRS, L])
        q = sb("q", [P, PAIRS, P])
        qrot = sb("qrot", [P, PAIRS, P])
        kraw = sb("kraw", [P, PAIRS, P])
        xT = sb("a_xT", [P, QB, P])
        oT = sb("oT", [P, PAIRS, P])
        xf = sb("a_xf", [P, D])
        y = sb("y", [P, D])
        mx = sb("mx", [P, TILES])
        nmx = sb("nmx", [P, TILES])
        sums = sb("sums", [P, TILES])
        rsum = sb("rsum", [P, TILES])
        krot = sb("krot", [P, PAIRS, P])
        q_tiled = oT
        dist = std[:, 0, :]
        mask = std[:, 1, :]
        ker = std[:, 2, :]

        p_up = ps("p_up", [P, 2, 2, L])
        p_down = ps("p_down", [P, 2, L])
        p_gap = ps("p_gap", [P, 2, L])

        zeroed = sem("a_zeroed")
        consts = sem("a_consts")
        pr_zeroed = sem("pr_zeroed")
        sp_abs = sem("sp_abs")
        sp_exp = sem("sp_exp")
        sp_ln = sem("sp_ln")
        sp_sum = sem("sp_sum")
        ker_ln = sem("ker_ln")
        ker_ready = sem("ker_ready")
        tables = sem("tables")
        ker_placed = sem("ker_placed")
        xT_loaded = [sem(f"xT_loaded{i}") for i in range(QB)]
        xf_loaded = sem("a_xf_loaded")
        rotq_loaded = sem("rotq_loaded")
        rotk_loaded = sem("rotk_loaded")
        ropeq = sem("ropeq")
        ropek = sem("ropek")
        qstep = sem("qstep")
        kstep = sem("kstep")
        x_loaded = [sem(f"x_loaded{i}") for i in range(RING)]
        sc_loaded = [sem(f"sc_loaded{i}") for i in range(RING)]
        up_done = sem("a_up_done")
        gelu_done = sem("a_gelu_done")
        down_done = sem("a_down_done")
        sc_ready = sem("sc_ready")
        logit_turn = sem("logit_turn")
        norm_turn = sem("norm_turn")
        load_turn = sem("load_turn")
        logit_done = sem("logit_done")
        nmx_ready = sem("nmx_ready")
        exp_done = sem("exp_done")
        rsum_ready = sem("rsum_ready")
        norm_done = sem("norm_done")
        gap_fill = sem("gap_fill")
        gap_read = sem("gap_read")
        y_stored = sem("y_stored")

        N_CONST = 7 + 2 * 2 * HALF + HALF + HALF + 3 * TQ
        PROLOGUE = 4 + H + 4

        def plan(last_batch):
            at, base = {}, 0
            for ib in range(QB):
                more = last_batch and ib == QB - 1
                more2 = last_batch and ib >= QB - 2
                for kind, count in (("scores", 0 if more else H), ("v", 2), ("qk", 0 if more2 else 4),
                                    ("t", (ib + 1) * QB), ("pv", 2), ("o", 1)):
                    at[ib, kind] = base
                    base += count
            return at, base

        UNITS, PER_BATCH = plan(False)
        UNITS_LAST, _ = plan(True)

        def unit(b, ib, kind, k=0):
            at = (UNITS_LAST if isinstance(b, int) else UNITS)[ib, kind] + k
            return PER_BATCH * b + (PROLOGUE + at), at % 2

        assert PER_BATCH % 2 == 0 and PROLOGUE % 2 == 0

        def over_batches(eng, step):
            with eng.Fori(0, B - 1) as b:
                for ib in range(QB):
                    step(b, ib, False)
            for ib in range(QB):
                step(B - 1, ib, True)

        def ahead(b, ib, m):
            return (b, ib + m) if ib + m < QB else (b + 1, ib + m - QB)

        def window(t):
            return slice(L - TQ * (t + 1), L)

        def tiled(a, apart):
            v = a[:].rearrange("p c (a n) -> p (c a) n", n=4 * TQ)
            return v.rearrange("p a (i b) -> p a b i", b=4) if apart else v.rearrange("p a (b i) -> p a b i", b=4)

        def wide(table):
            return table.unsqueeze(1).broadcast_to([P, PAIRS, P])

        block = ctx.enter_context(nc.Block())

        @block.sync
        def _(sp):
            sp.dma_start(wqkv[:], w_qkv).then_inc(consts, 16)
            sp.dma_start(xT[:, 0, :], xnT_dram[0, :, 0:P]).then_inc(xT_loaded[0], 16)
            sp.dma_start(xT[:, 1, :], xnT_dram[0, :, P:2 * P]).then_inc(xT_loaded[1], 16)
            sp.dma_start(cos[:], c["c_cos"]).then_inc(consts, 16)
            sp.dma_start(sin[:], c["c_sin"]).then_inc(consts, 16)
            sp.dma_start(dist, c["c_dist"]).then_inc(consts, 16)
            sp.dma_start(mask, c["c_mask"]).then_inc(consts, 16)
            sp.dma_start(ident[:], c["c_ident"]).then_inc(consts, 16)
            for i in range(TQ):
                r = slice(i * H, (i + 1) * H)
                sp.dma_start(cols[r, 0:1], log_p).then_inc(consts, 16)
                sp.dma_start(cols[r, 1:2], log_a).then_inc(consts, 16)
                sp.dma_start(cols[r, 2:3], b2.rearrange("(n a) -> n a", a=1)).then_inc(consts, 16)
            sp.wait_ge(zeroed, 1)
            for i in range(HALF):
                sp.dma_start(cols[i * C:(i + 1) * C, 3:4], b1.rearrange("(n a) -> n a", a=1)).then_inc(consts, 16)
                sp.dma_start(w_down[i * C:(i + 1) * C, i * H:(i + 1) * H], w2).then_inc(consts, 16)
                for half in range(2):
                    for kind in range(2):
                        r = HH * (half ^ kind) + i * H
                        sp.dma_start(w_up[r:r + H, half, i * C:(i + 1) * C], w1[kind * H:(kind + 1) * H, :])\
                            .then_inc(consts, 16)
            sp.dma_start(wo[:], w_o.rearrange("(c k) n -> k c n", k=P)).then_inc(consts, 16)
            sp.wait_ge(ker_ready, 1)
            for r in range(RING):
                sp.dma_start(xa[HH:, 0, r, :], ker[:HH, :]).then_inc(ker_placed, 16)
                sp.dma_start(xa[:HH, 1, r, :], ker[HH:, :]).then_inc(ker_placed, 16)
            sp.wait_ge(ker_placed, 16 * 2 * RING)

            def rotate():
                for raw, rot, loaded in ((q, qrot, rotq_loaded), (kraw, krot, rotk_loaded)):
                    for h in range(4):
                        to, fr = h * 32, (h ^ 1) * 32
                        sp.dma_start(rot[to:to + 32], raw[fr:fr + 32]).then_inc(loaded, 16)

            def tile(b, ib, t):
                g = 64 * b + (16 * ib + t)
                r, w = t % RING, window(16 * ib + t)
                n_keys = TQ * (16 * ib + t + 1)
                row = 32 * (t // 4) + t % 4
                sp.wait_ge(up_done, g + 1)
                for half in range(2):
                    fr = row + 16 * half
                    sp.dma_start(xa[HH * half:HH * half + HH, half, r, w], std[fr:fr + 13:4, :, 0:n_keys])\
                        .then_inc(x_loaded[r], 16)
                sp.wait_ge(logit_done, g + 1)
                sp.dma_start(sc[:, r, w], std[row:row + 29:4, :, 0:n_keys]).then_inc(sc_loaded[r], 16)

            sp.sem_inc(y_stored, 16)
            sp.wait_ge(gap_read, 4 + 2)
            rotate()
            sp.wait_ge(gap_read, 4 + H + 2)
            for t in range(RING):
                tile(0, 0, t)
            sp.wait_ge(gap_read, PROLOGUE + 2)

            out_rows = out.rearrange("(b k p) n -> b k p n", k=QB, p=P)
            xf_rows = xf_dram.rearrange("(b k p) n -> b k p n", k=QB, p=P)

            def step(b, ib, last):
                if not (last and ib == QB - 1):
                    rotate()
                if not (last and ib >= QB - 2):
                    bn, ibn = ahead(b, ib, 2)
                    sp.dma_start(xT[:, ibn, :], xnT_dram[bn, :, ibn * P:(ibn + 1) * P]).then_inc(xT_loaded[ibn], 16)
                sp.dma_start(xf[:], xf_rows[b, ib]).then_inc(xf_loaded, 16)
                for t in range(RING, TILES):
                    tile(b, ib, t)
                if not (last and ib == QB - 1):
                    sp.wait_ge(gap_read, unit(b, ib, "scores", H)[0] + 2)
                    sp.sem_inc(load_turn, 1)
                    for t in range(RING):
                        tile(*ahead(b, ib, 1), t)
                sp.wait_ge(gap_read, unit(b, ib, "o")[0] + 1 + 2)
                sp.dma_start(out_rows[b, ib], y[:]).then_inc(y_stored, 16)

            over_batches(sp, step)
            sp.wait_ge(y_stored, 16 * BLOCKS + 16)

        @block.gpsimd
        def _(pool):
            nc.gpsimd.memset(w_up[:], 0.0)
            nc.gpsimd.memset(w_down[:], 0.0).then_inc(zeroed, 1)
            nc.gpsimd.memset(pr[:], 0.0).then_inc(pr_zeroed, 1)
            pool.wait_ge(tables, 1)
            steps = [0]

            def rope_keys(b, ib):
                m = 4 * b + ib
                cs = slice(ib * P, (ib + 1) * P)
                pool.wait_ge(rotk_loaded, 64 * m + 64)
                nc.gpsimd.tensor_tensor(kraw[:], kraw[:], wide(cos[:, cs]), ALU.mult).then_inc(kstep, 1)
                nc.gpsimd.tensor_tensor(krot[:], krot[:], wide(sin[:, cs]), ALU.mult).then_inc(kstep, 1)
                pool.wait_ge(kstep, 2 * m + 2)
                nc.gpsimd.tensor_tensor(kk[:, :, cs], kraw[:], krot[:], ALU.add).then_inc(ropek, 1)

            rope_keys(0, 0)

            def step(b, ib, last):
                for t in range(TILES):
                    g = 64 * b + (16 * ib + t)
                    w = window(16 * ib + t)
                    pool.wait_ge(sc_loaded[t % RING], 16 * (16 * b + (4 * ib + t // RING)) + 16)
                    nc.gpsimd.tensor_tensor(sc[:, t % RING, w], sc[:, t % RING, w], ker_mask[:, w], ALU.add)\
                        .then_inc(sc_ready, 1)
                    if t == 5 and not (last and ib == QB - 1):
                        rope_keys(*ahead(b, ib, 1))
                for t in range(TILES):
                    if t % 4 == 0:
                        pool.wait_ge(rsum_ready, 16 * b + (4 * ib + t // 4) + 1)
                        pool.sem_inc(norm_turn, 1)
                    w = slice(L - (ib + 1) * P, L - P + TQ * (t + 1))
                    nc.gpsimd.tensor_scalar(pr[:, t, w], pr[:, t, w], rsum[:, t:t + 1], None, ALU.mult)\
                        .then_inc(norm_done, 1)

            over_batches(pool, step)

        @block.scalar
        def _(act):
            act.sem_inc(gelu_done, 2)
            act.wait_ge(consts, 16 * N_CONST)
            act.wait_ge(sp_abs, 1)
            nc.scalar.activation(cols[:, 6:8], cols[:, 4:6], ACT.Exp, scale=-1.0).then_inc(sp_exp, 1)
            act.wait_ge(sp_exp, 1)
            nc.scalar.activation(cols[:, 8:10], cols[:, 6:8], ACT.Ln, bias=1.0).then_inc(sp_ln, 1)
            act.wait_ge(sp_sum, 1)
            nc.scalar.activation(ker, dist, ACT.Ln, bias=1.0, scale=cols[:, 11:12]).then_inc(ker_ln, 1)

            def step(b, ib, last):
                for t in range(TILES):
                    g = 64 * b + (16 * ib + t)
                    n_keys = TQ * (16 * ib + t + 1)
                    act.wait_ge(down_done, g + 1)
                    act.wait_ge(up_done, g + 1 + RING)
                    nc.scalar.activation(hid[:, t % 2, :, 0:n_keys], p_up[:, t % 2, :, 0:n_keys], ACT.Gelu,
                                         bias=cols[:, 3:4]).then_inc(gelu_done, 1)
                act.wait_ge(nmx_ready, 4 * b + ib + 1)
                for t in range(TILES):
                    w = slice(L - (ib + 1) * P, L - P + TQ * (t + 1))
                    nc.scalar.activation(pr[:, t, w], pr[:, t, w], ACT.Exp, bias=nmx[:, t:t + 1],
                                         accum_out=sums[:, t:t + 1]).then_inc(exp_done, 1)

            over_batches(act, step)

        @block.vector
        def _(dve):
            dve.sem_inc(logit_done, RING)
            dve.sem_inc(gap_read, 2)
            dve.wait_ge(consts, 16 * N_CONST)
            nc.vector.scalar_tensor_tensor(out=cols[:, 4:6], in0=cols[:, 0:2], scalar=-1.0, in1=cols[:, 0:2],
                                           op0=ALU.mult, op1=ALU.max).then_inc(sp_abs, 1)
            dve.wait_ge(sp_ln, 1)
            nc.vector.scalar_tensor_tensor(out=cols[:, 10:12], in0=cols[:, 0:2], scalar=0.0, in1=cols[:, 8:10],
                                           op0=ALU.max, op1=ALU.add).then_inc(sp_sum, 1)
            dve.wait_ge(ker_ln, 1)
            nc.vector.tensor_scalar(ker, ker, cols[:, 10:11], -1.0, ALU.mult, ALU.mult).then_inc(ker_ready, 1)
            dve.wait_ge(ker_ready, 1)
            nc.vector.scalar_tensor_tensor(out=ker_mask[:], in0=ker, scalar=cols[:, 2:3], in1=mask,
                                           op0=ALU.add, op1=ALU.add).then_inc(tables, 1)

            dve.wait_ge(pr_zeroed, 1)

            def scores_read(at, ib, after=lambda h: None):
                w = slice(0, (ib + 1) * P)
                for h in range(H):
                    k, bank = at(h)
                    dve.wait_ge(gap_fill, k + 1)
                    nc.vector.tensor_scalar(std[:, h, w], p_gap[:, bank, w], HD ** -0.5, None, ALU.mult)\
                        .then_inc(gap_read, 1)
                    after(h)

            def qk_read(at, m):
                for j in range(4):
                    k, bank = at(j)
                    if j == 2 and (not isinstance(m, int) or m):
                        dve.wait_ge(ropek, m)
                    dve.wait_ge(gap_fill, k + 1)
                    nc.vector.tensor_copy((q, kraw)[j // 2][:, (j % 2) * 4:(j % 2) * 4 + 4, :],
                                          p_gap[:, bank, :].rearrange("p (c n) -> p c n", n=P)).then_inc(gap_read, 1)

            def rope_queries(b, ib):
                m = 4 * b + ib
                cs = slice(ib * P, (ib + 1) * P)
                dve.wait_ge(rotq_loaded, 64 * m + 64)
                nc.vector.tensor_tensor(q[:], q[:], wide(cos[:, cs]), ALU.mult).then_inc(qstep, 1)
                nc.vector.tensor_tensor(qrot[:], qrot[:], wide(sin[:, cs]), ALU.mult).then_inc(qstep, 1)
                dve.wait_ge(qstep, 2 * m + 2)
                nc.vector.tensor_tensor(tiled(q_tiled, True), tiled(q, False), tiled(qrot, False), ALU.add)\
                    .then_inc(ropeq, 1)

            qk_read(lambda j: (j, j % 2), 0)
            rope_queries(0, 0)
            dve.wait_ge(ker_placed, 16 * 2 * RING)
            dve.wait_ge(tables, 1)
            scores_read(lambda j: (4 + j, j % 2), 0)
            qk_read(lambda j: (4 + H + j, j % 2), 1)

            def step(b, ib, last):
                n = 4 * b + ib
                for t in range(TILES):
                    g = 64 * b + (16 * ib + t)
                    n_keys = TQ * (16 * ib + t + 1)
                    dve.wait_ge(down_done, g + 1 + 2)
                    dve.wait_ge(sc_ready, g + 1)
                    dve.sem_inc(logit_turn, 1)
                    w = slice(L - (ib + 1) * P, L - P + TQ * (t + 1))
                    nc.vector.tensor_tensor_reduce(
                        out=pr[:, t, w], in0=p_down[:, t % 2, 0:n_keys], in1=sc[:, t % RING, window(16 * ib + t)],
                        scale=1.0, scalar=-3e38, op0=ALU.add, op1=ALU.max, accum_out=mx[:, t:t + 1])\
                        .then_inc(logit_done, 1)
                    if t == 5 and not (last and ib == QB - 1):
                        rope_queries(*ahead(b, ib, 1))
                dve.wait_ge(logit_done, 64 * b + (16 * ib + 16) + RING)
                nc.vector.tensor_scalar(nmx[:], mx[:], -1.0, None, ALU.mult).then_inc(nmx_ready, 1)

                def inverse_sums(j):
                    dve.wait_ge(exp_done, 64 * b + (16 * ib + 4 * j + 4))
                    nc.vector.reciprocal(rsum[:, 4 * j:4 * j + 4], sums[:, 4 * j:4 * j + 4]).then_inc(rsum_ready, 1)

                at_h = {9: 0, 12: 1, 15: 2}
                if not (last and ib == QB - 1):
                    scores_read(lambda j: unit(b, ib, "scores", j), (ib + 1) % QB,
                                lambda h: inverse_sums(at_h[h]) if h in at_h else None)
                else:
                    for j in range(3):
                        inverse_sums(j)
                for j in range(2):
                    k, bank = unit(b, ib, "v", j)
                    dve.wait_ge(gap_fill, k + 1)
                    nc.vector.tensor_copy(vv[:, ib, j * L:(j + 1) * L], p_gap[:, bank, :]).then_inc(gap_read, 1)
                inverse_sums(3)
                if not (last and ib >= QB - 2):
                    qk_read(lambda j: unit(b, ib, "qk", j), n + 2)
                for j in range((ib + 1) * QB):
                    four, kb = divmod(j, ib + 1)
                    k, bank = unit(b, ib, "t", j)
                    dve.wait_ge(gap_fill, k + 1)
                    nc.vector.tensor_copy(pT[:, kb, :, 4 * TQ * four:4 * TQ * (four + 1)],
                                          p_gap[:, bank, :].rearrange("p (i h) -> p h i", h=H)).then_inc(gap_read, 1)
                for j in range(2):
                    k, bank = unit(b, ib, "pv", j)
                    dve.wait_ge(gap_fill, k + 1)
                    nc.vector.tensor_copy(oT[:, 4 * j:4 * j + 4, :],
                                          p_gap[:, bank, :].rearrange("p (c n) -> p c n", n=P)).then_inc(gap_read, 1)
                k, bank = unit(b, ib, "o")
                dve.wait_ge(y_stored, 16 * n + 16)
                dve.wait_ge(xf_loaded, 16 * n + 16)
                dve.wait_ge(gap_fill, k + 1)
                nc.vector.tensor_tensor(y[:], p_gap[:, bank, 0:D], xf[:], ALU.add).then_inc(gap_read, 1)

            over_batches(dve, step)

        @block.tensor
        def _(pe):
            pe.sem_inc(up_done, RING)
            pe.sem_inc(down_done, 2)
            pe.wait_ge(consts, 16 * N_CONST)

            def qk_unit(at, j, b, ib):
                k, bank = at(j)
                if j == 0:
                    pe.wait_ge(xT_loaded[ib], 16 * b + 16)
                pe.wait_ge(gap_read, k + 1)
                for i in range(4):
                    m = 4 * j + i
                    last_mm = nc.tensor.matmul(p_gap[:, bank, i * P:(i + 1) * P], wqkv[:, m * P:(m + 1) * P],
                                               xT[:, ib, :], start=True, stop=True)
                last_mm.then_inc(gap_fill, 1)

            def scores_unit(at, h, b, ib):
                k, bank = at(h)
                if h == 0:
                    pe.wait_ge(ropeq, 4 * b + ib + 1)
                    pe.wait_ge(ropek, 4 * b + ib + 1)
                r = slice(HD * (h % 2), HD * (h % 2) + HD)
                n_keys = (ib + 1) * P
                pe.wait_ge(gap_read, k + 1)
                nc.tensor.matmul(p_gap[:, bank, 0:n_keys],
                                 q_tiled[r, h // 2, :], kk[r, h // 2, 0:n_keys], start=True, stop=True).then_inc(gap_fill, 1)

            for j in range(4):
                qk_unit(lambda j: (j, j % 2), j, 0, 0)
            for h in range(H):
                scores_unit(lambda j: (4 + j, j % 2), h, 0, 0)
            for j in range(4):
                qk_unit(lambda j: (4 + H + j, j % 2), j, 0, 1)
            pe.wait_ge(ker_placed, 16 * 2 * RING)

            def step(b, ib, last):
                def up(t):
                    g = 64 * b + (16 * ib + t)
                    r = t % RING
                    n_keys = TQ * (16 * ib + t + 1)
                    pe.wait_ge(gelu_done, g + 1)
                    pe.wait_ge(x_loaded[r], 32 * (16 * b + (4 * ib + t // RING)) + 32)
                    for half in range(2):
                        last_mm = nc.tensor.matmul(p_up[:, t % 2, half, 0:n_keys], w_up[:, half, :],
                                                   xa[:, half, r, window(16 * ib + t)], start=True, stop=True)
                    last_mm.then_inc(up_done, 1)

                def down(t):
                    g = 64 * b + (16 * ib + t)
                    n_keys = TQ * (16 * ib + t + 1)
                    pe.wait_ge(logit_done, g + 1 + 2)
                    pe.wait_ge(gelu_done, g + 1 + 2)
                    for half in range(2):
                        last_mm = nc.tensor.matmul(p_down[HH * half:HH * half + HH, t % 2, 0:n_keys], w_down[:],
                                                   hid[:, t % 2, half, 0:n_keys], start=True, stop=True)
                    last_mm.then_inc(down_done, 1)

                for t in range(TILES):
                    up(t)
                    if t:
                        down(t - 1)
                more = not (last and ib == QB - 1)
                for h in range(H if more else 0):
                    scores_unit(lambda j: unit(b, ib, "scores", j), h, *ahead(b, ib, 1))
                    if h == 1:
                        down(TILES - 1)
                if not more:
                    down(TILES - 1)
                for j in range(2):
                    k, bank = unit(b, ib, "v", j)
                    pe.wait_ge(gap_read, k + 1)
                    v0 = 2 * H * HD + j * L
                    nc.tensor.matmul(p_gap[:, bank, :], xT[:, ib, :], wqkv[:, v0:v0 + L], start=True, stop=True)\
                        .then_inc(gap_fill, 1)
                if not (last and ib >= QB - 2):
                    for j in range(4):
                        qk_unit(lambda j: unit(b, ib, "qk", j), j, *ahead(b, ib, 2))
                for j in range((ib + 1) * QB):
                    four, kb = divmod(j, ib + 1)
                    k, bank = unit(b, ib, "t", j)
                    pe.wait_ge(norm_done, 64 * b + (16 * ib + 4 * four + 4))
                    pe.wait_ge(gap_read, k + 1)
                    c0 = L - (ib + 1 - kb) * P
                    for i in range(4):
                        last_mm = nc.tensor.transpose(p_gap[:, bank, i * P:(i + 1) * P],
                                                      pr[:, 4 * four + i, c0:c0 + P], ident[:])
                    last_mm.then_inc(gap_fill, 1)
                pe.wait_ge(gap_read, unit(b, ib, "pv")[0] + 2)
                for j in range(2):
                    k, bank = unit(b, ib, "pv", j)
                    for i in range(4):
                        for kb in range(ib + 1):
                            for r in range(2):
                                h = 2 * (4 * j + i) + r
                                last_mm = nc.tensor.matmul(
                                    p_gap[HD * r:HD * r + HD, bank, i * P:(i + 1) * P],
                                    vv[:, kb, h * HD:(h + 1) * HD], pT[:, kb, h, :],
                                    start=(kb == 0), stop=(kb == ib))
                    last_mm.then_inc(gap_fill, 1)
                k, bank = unit(b, ib, "o")
                pe.wait_ge(gap_read, k + 2)
                for i in range(PAIRS):
                    last_mm = nc.tensor.matmul(p_gap[:, bank, 0:D], oT[:, i, :], wo[:, i, :],
                                               start=(i == 0), stop=(i == PAIRS - 1))
                last_mm.then_inc(gap_fill, 1)

            over_batches(pe, step)


def build(nc, a, c, out):
    xnT_dram = nc.dram_tensor("xnT_scratch", [CHUNKS, D, CH], F32, kind="Internal").ap()
    gT_dram = nc.dram_tensor("gT_scratch", [CHUNKS, P, CH], F32, kind="Internal").ap()
    xf_dram = nc.dram_tensor("xf_scratch", [ROWS, D], F32, kind="Internal").ap()
    x = a["L0_attn_x"].rearrange("b l d -> (b l) d")
    heads = lambda v: v.rearrange("h a b -> h (a b)")
    norm_and_gates(nc, x, a["L0_ffn_Wm"], a["L0_ffn_bm"], a["L0_ffn_expert_emb"], c, xnT_dram, gT_dram)
    experts(nc, x, a["L0_ffn_Wm"], a["L0_ffn_bm"], a["L0_ffn_W1"], a["L0_ffn_b1"], a["L0_ffn_W2"], a["L0_ffn_b2"],
            a["L0_ffn_Wo"], a["L0_ffn_bo"], c, xnT_dram, gT_dram, xf_dram)
    attention(nc, a["L0_attn_w_qkv"], a["L0_attn_w_o"], heads(a["L0_attn_log_p"]), heads(a["L0_attn_log_a"]),
              a["L0_attn_w1"], a["L0_attn_b1"], a["L0_attn_w2"], a["L0_attn_b2"], c, xnT_dram, xf_dram,
              out.rearrange("b l d -> (b l) d"))


_INS = ["L0_attn_x", "L0_attn_w_qkv", "L0_attn_w_o", "L0_attn_log_p", "L0_attn_log_a", "L0_attn_w1", "L0_attn_b1",
        "L0_attn_w2", "L0_attn_b2", "L0_ffn_Wm", "L0_ffn_bm", "L0_ffn_expert_emb", "L0_ffn_W1", "L0_ffn_b1",
        "L0_ffn_W2", "L0_ffn_b2", "L0_ffn_Wo", "L0_ffn_bo"]


def kernel(**inputs):
    import numpy as _np
    import concourse.bacc as _bacc
    from concourse import mybir as _mybir
    from concourse.bass_utils import run_bass_kernel_spmd as _run

    nc = _bacc.Bacc("TRN2", target_bir_lowering=False, num_devices=1)
    arrays, args, consts = {}, {}, {}
    for name in _INS:
        a = _np.ascontiguousarray(inputs[name])
        arrays[f"in_{name}"] = a
        args[name] = nc.dram_tensor(f"in_{name}", a.shape, _mybir.dt.from_np(a.dtype), kind="ExternalInput").ap()
    for name, a in shape_constants().items():
        a = _np.ascontiguousarray(a)
        arrays[name] = a
        consts[name] = nc.dram_tensor(name, a.shape, _mybir.dt.from_np(a.dtype), kind="ExternalInput").ap()
    out = nc.dram_tensor("out_0", (B, L, D), _mybir.dt.float32, kind="ExternalOutput").ap()
    build(nc, args, consts, out)
    r = _run(nc, [arrays], core_ids=[0])
    return r.results[0]["out_0"]
```

```python
from contextlib import ExitStack

import numpy as np

import concourse.bass as bass
from concourse import mybir

F32 = mybir.dt.float32
F32R = mybir.dt.float32r
ALU = mybir.AluOpType
ACT = mybir.ActivationFunctionType
AX = mybir.AxisListType.X

P = 128
B, L, D = 8, 512, 128
ROWS = B * L
BLOCKS = ROWS // P
H, HD = 16, 64
C = 2 * H
PAIRS = H // 2
QB = L // P
TQ = 8
TILES = P // TQ
HALF = TQ // 2
GT = 8
RING = 8
GROUPS = TILES // GT
GQ = GT * TQ
LAG = 2
HIDS = LAG + 1
S, SD = 8, 16
E, I = 16, 64
EP = E // 2
CH = 512
CHUNKS = ROWS // CH
EPS = 1e-5
MASKED = -1e30


def shape_constants():
    f = np.float32
    inv_freq = (f(1.0) / np.power(f(10000.0), np.arange(0, HD, 2, dtype=f) / f(HD))).astype(f)
    freqs = np.outer(np.arange(L, dtype=f), inv_freq).astype(f)
    emb = np.concatenate([freqs, freqs], -1)
    cos, sin = np.cos(emb).astype(f).T, np.sin(emb).astype(f).T
    sign = np.where(np.arange(HD) < HD // 2, f(-1), f(1))[:, None]
    cols = np.arange(L) - (L - TQ)
    dist = (np.arange(P) // H)[:, None] - cols[None]
    e_rev = np.broadcast_to((E - np.arange(E)).astype(f), (P, BLOCKS * S, E))
    k = np.arange(P)
    sel = np.zeros((P, S, 2, P), f)
    for s in range(S):
        for half in range(2):
            want = s * E + half * (E // 2) + k // SD
            sel[want, s, half, k] = 1
    return {
        "c_ident": np.eye(P, dtype=f),
        "c_cos": np.concatenate([cos, cos]),
        "c_sin": np.concatenate([sin * sign, sin * sign]),
        "c_dist": np.abs(dist).astype(f),
        "c_mask": np.where(dist < 0, f(MASKED), f(0)),
        "c_erev": np.ascontiguousarray(e_rev[:, 0]),
        "c_sel": sel.reshape(P, S * 2 * P),
    }


def norm_and_gates(nc, x, Wm, bm, emb, c, xnT_dram, gT_dram):
    with ExitStack() as ctx:
        def sb(name, shape, dt=F32):
            return ctx.enter_context(nc.sbuf_tensor(name, shape, dt))

        def ps(name, shape):
            return ctx.enter_context(nc.psum_tensor(name, shape, F32))

        def sem(name):
            return ctx.enter_context(nc.semaphore(name))

        G = BLOCKS * S
        x_all = sb("x_all", [P, BLOCKS, D])
        ident = sb("n_ident", [P, P])
        wm = sb("n_wm", [D, D])
        bmc = sb("n_bmc", [D, 1])
        emb_bd = sb("emb_bd", [P, P])
        erev = sb("erev", [P, E])
        stats = sb("stats", [P, BLOCKS, 6])
        small = sb("n_small", [P, 5, BLOCKS])
        xn = sb("xn", [P, 4, P])
        xT = sb("n_xT", [P, CH])
        hT = sb("n_hT", [P, CH])
        logit = sb("logit", [P, G, E])
        ex = sb("ex", [P, G, E])
        t1 = sb("t1", [P, G, E])
        first = sb("first", [P, G, E])
        red = sb("red", [P, 6, G])
        gT = sb("n_gT", [P, CH])
        pT = ps("n_pT", [P, CH])
        pH = ps("n_pH", [P, CH])
        pL = ps("n_pL", [P, CH])
        pG = ps("n_pG", [P, CH])

        zeroed = sem("n_zeroed")
        consts = sem("n_consts")
        x_loaded = sem("x_loaded")
        step = sem("n_step")
        var_ready = sem("var_ready")
        std_ready = sem("std_ready")
        xn_ready = sem("xn_ready")
        xT_psum = sem("xT_psum")
        xT_ready = sem("xT_ready")
        xT_stored = sem("xT_stored")
        hT_psum = sem("hT_psum")
        hT_ready = sem("hT_ready")
        lg_psum = sem("lg_psum")
        lg_ready = sem("lg_ready")
        diff_ready = sem("diff_ready")
        ex_ready = sem("ex_ready")
        gates_ready = sem("gates_ready")
        gT_psum = sem("gT_psum")
        gT_ready = sem("gT_ready")
        gT_stored = sem("gT_stored")

        N_CONST = 4 + S
        bc = lambda a: a.unsqueeze(2).broadcast_to([P, G, E])

        block = ctx.enter_context(nc.Block())

        @block.sync
        def _(sp):
            sp.sem_inc(xT_stored, 16)
            sp.sem_inc(gT_stored, 16)
            sp.dma_start(x_all[:], x.rearrange("(k p) n -> p k n", p=P)).then_inc(x_loaded, 16)
            sp.dma_start(ident[:], c["c_ident"]).then_inc(consts, 16)
            sp.dma_start(wm[:], Wm).then_inc(consts, 16)
            sp.dma_start(bmc[:], bm.rearrange("(n a) -> n a", a=1)).then_inc(consts, 16)
            sp.dma_start(erev[:], c["c_erev"]).then_inc(consts, 16)
            sp.wait_ge(zeroed, 1)
            for s in range(S):
                sp.dma_start(emb_bd[s * SD:(s + 1) * SD, s * E:(s + 1) * E], emb).then_inc(consts, 16)
            with sp.Fori(0, CHUNKS) as i:
                sp.wait_ge(xT_ready, i + 2)
                sp.dma_start(xnT_dram[i], xT[:]).then_inc(xT_stored, 16)
            with sp.Fori(0, CHUNKS) as i:
                sp.wait_ge(gT_ready, i + 1)
                sp.dma_start(gT_dram[i], gT[:]).then_inc(gT_stored, 16)
            sp.wait_ge(xT_stored, 16 * CHUNKS + 16)
            sp.wait_ge(gT_stored, 16 * CHUNKS + 16)

        @block.gpsimd
        def _(pool):
            nc.gpsimd.memset(emb_bd[:], 0.0).then_inc(zeroed, 1)

        @block.vector
        def _(dve):
            done = [0]

            def link(ins):
                done[0] += 1
                ins.then_inc(step, 1)
                dve.wait_ge(step, done[0])

            dve.sem_inc(lg_ready, 1)
            dve.wait_ge(x_loaded, 16)
            with dve.Fori(0, BLOCKS - 1) as k:
                nc.vector.bn_stats(stats[:, k, :], x_all[:, k, :])
            link(nc.vector.bn_stats(stats[:, BLOCKS - 1, :], x_all[:, BLOCKS - 1, :]))
            mean, var, dm, rstd, nmr = (small[:, j, :] for j in range(5))
            link(nc.vector.tensor_tensor(mean, stats[:, :, 1], stats[:, :, 4], ALU.add))
            link(nc.vector.tensor_tensor(dm, stats[:, :, 1], stats[:, :, 4], ALU.subtract))
            link(nc.vector.tensor_tensor(dm, dm, dm, ALU.mult))
            link(nc.vector.tensor_tensor(var, stats[:, :, 2], stats[:, :, 5], ALU.add))
            link(nc.vector.tensor_scalar(var, var, 1.0 / D, EPS, ALU.mult, ALU.add))
            nc.vector.scalar_tensor_tensor(out=var, in0=dm, scalar=0.25, in1=var, op0=ALU.mult,
                                           op1=ALU.add).then_inc(var_ready, 1)
            dve.wait_ge(std_ready, 1)
            link(nc.vector.reciprocal(rstd, rstd))
            link(nc.vector.scalar_tensor_tensor(out=nmr, in0=mean, scalar=-0.5, in1=rstd, op0=ALU.mult,
                                                op1=ALU.mult))
            with dve.Fori(0, CHUNKS) as i:
                dve.wait_ge(xT_psum, i + 1)
                for j in range(4):
                    last = nc.vector.tensor_scalar(xn[:, j, :], x_all[:, i * 4 + j, :],
                                                   small[:, 3, bass.ds(i * 4 + j, 1)],
                                                   small[:, 4, bass.ds(i * 4 + j, 1)], ALU.mult, ALU.add)
                last.then_inc(xn_ready, 1)
                dve.wait_ge(lg_psum, i + 2)
                nc.vector.tensor_copy(logit[:, bass.ds(i * (4 * S), 4 * S), :],
                                      pL[:].rearrange("p (g e) -> p g e", e=E)).then_inc(lg_ready, 1)
            dve.wait_ge(lg_ready, CHUNKS + 1)
            rmax, ridx, rmax2, ridx2, rsum, rinv = (red[:, j, :] for j in range(6))
            erev_b = erev[:].unsqueeze(1).broadcast_to([P, G, E])
            link(nc.vector.tensor_reduce(rmax, logit[:], AX, ALU.max))
            nc.vector.tensor_tensor(logit[:], logit[:], bc(rmax), ALU.subtract).then_inc(diff_ready, 1)
            dve.wait_ge(diff_ready, 1)
            link(nc.vector.scalar_tensor_tensor(out=t1[:], in0=logit[:], scalar=0.0, in1=erev_b,
                                                op0=ALU.is_equal, op1=ALU.mult))
            link(nc.vector.tensor_reduce(ridx, t1[:], AX, ALU.max))
            link(nc.vector.tensor_tensor(first[:], t1[:], bc(ridx), ALU.is_equal))
            dve.wait_ge(ex_ready, 1)
            link(nc.vector.scalar_tensor_tensor(out=logit[:], in0=first[:], scalar=MASKED, in1=logit[:],
                                                op0=ALU.mult, op1=ALU.add))
            link(nc.vector.tensor_reduce(rmax2, logit[:], AX, ALU.max))
            link(nc.vector.tensor_tensor(t1[:], logit[:], bc(rmax2), ALU.is_equal))
            link(nc.vector.tensor_tensor(t1[:], t1[:], erev_b, ALU.mult))
            link(nc.vector.tensor_reduce(ridx2, t1[:], AX, ALU.max))
            link(nc.vector.tensor_tensor(t1[:], t1[:], bc(ridx2), ALU.is_equal))
            link(nc.vector.tensor_tensor(first[:], first[:], t1[:], ALU.add))
            link(nc.vector.tensor_reduce(rsum, ex[:], AX, ALU.add))
            link(nc.vector.reciprocal(rinv, rsum))
            link(nc.vector.tensor_tensor(ex[:], ex[:], first[:], ALU.mult))
            nc.vector.tensor_tensor(ex[:], ex[:], bc(rinv), ALU.mult).then_inc(gates_ready, 1)

        @block.scalar
        def _(act):
            act.sem_inc(xT_ready, 1)
            act.sem_inc(hT_ready, 1)
            act.wait_ge(var_ready, 1)
            nc.scalar.activation(small[:, 3, :], small[:, 1, :], ACT.Sqrt).then_inc(std_ready, 1)
            act.wait_ge(consts, 16 * N_CONST)
            with act.Fori(0, CHUNKS) as i:
                act.wait_ge(xT_stored, i * 16 + 16)
                act.wait_ge(xT_psum, i + 2)
                nc.scalar.activation(xT[:], pT[:], ACT.Copy).then_inc(xT_ready, 1)
                act.wait_ge(lg_psum, i + 1)
                act.wait_ge(hT_psum, i + 1)
                nc.scalar.activation(hT[:], pH[:], ACT.Identity, bias=bmc[:]).then_inc(hT_ready, 1)
            act.wait_ge(diff_ready, 1)
            nc.scalar.activation(ex[:], logit[:], ACT.Exp).then_inc(ex_ready, 1)
            with act.Fori(0, CHUNKS) as i:
                act.wait_ge(gT_stored, i * 16 + 16)
                act.wait_ge(gT_psum, i + 1)
                nc.scalar.activation(gT[:], pG[:], ACT.Copy).then_inc(gT_ready, 1)

        @block.tensor
        def _(pe):
            pe.sem_inc(xT_psum, 1)
            pe.sem_inc(lg_psum, 1)
            pe.wait_ge(consts, 16 * N_CONST)
            with pe.Fori(0, CHUNKS) as i:
                pe.wait_ge(xT_ready, i + 1)
                pe.wait_ge(xn_ready, i + 1)
                for j in range(4):
                    last = nc.tensor.transpose(pT[:, j * P:(j + 1) * P], xn[:, j, :], ident[:])
                last.then_inc(xT_psum, 1)
                pe.wait_ge(hT_ready, i + 1)
                pe.wait_ge(xT_ready, i + 2)
                nc.tensor.matmul(pH[:], wm[:], xT[:], start=True, stop=True).then_inc(hT_psum, 1)
                pe.wait_ge(lg_ready, i + 1)
                pe.wait_ge(hT_ready, i + 2)
                for j in range(4):
                    last = nc.tensor.matmul(pL[:, j * P:(j + 1) * P], hT[:, j * P:(j + 1) * P], emb_bd[:],
                                            start=True, stop=True)
                last.then_inc(lg_psum, 1)
            pe.wait_ge(gates_ready, 1)
            for i in range(CHUNKS):
                if i:
                    pe.wait_ge(gT_ready, i)
                for j in range(4):
                    k = 4 * i + j
                    last = nc.tensor.transpose(pG[:, j * P:(j + 1) * P],
                                               ex[:, k * S:(k + 1) * S, :].rearrange("p g e -> p (g e)"), ident[:])
                last.then_inc(gT_psum, 1)


def experts(nc, x, Wm, bm, W1, b1, W2, b2, Wo, bo, c, xnT_dram, gT_dram, xf_dram):
    with ExitStack() as ctx:
        def sb(name, shape, dt=F32):
            return ctx.enter_context(nc.sbuf_tensor(name, shape, dt))

        def ps(name, shape):
            return ctx.enter_context(nc.psum_tensor(name, shape, F32))

        def sem(name):
            return ctx.enter_context(nc.semaphore(name))

        PARTS = 4
        SP = S // 2
        Q = 2 * SD
        UNITS = 2 * S
        EU = EP // 2
        HB, AB = 2, 4

        ident = sb("e_ident", [P, P])
        wm_rep = sb("wm_rep", [D, SP, PARTS, Q])
        bm_rep = sb("bm_rep", [P, SP])
        w1f = sb("w1f", [P, 2, E * I])
        w1r = sb("w1r", [P, 2, EP, 2 * I], F32R)
        b1c = sb("b1c", [P, EP])
        w2p = sb("w2p", [P, EP, 2 * SD])
        b2c = sb("b2c", [P, 2])
        wo_rep = sb("wo_rep", [P, S, D])
        boc = sb("boc", [P, 1])
        self_ = sb("self", [P, UNITS, P])
        selr = sb("selr", [P, UNITS, P], F32R)
        xT = sb("e_xT", [P, CH])
        gT = sb("e_gT", [P, CH])
        xr = sb("e_xr", [P, CH // P, D])
        tt = sb("tt", [P, CH])
        tr = sb("tr", [P, 2, SP, CH], F32R)
        g_hi = sb("g_hi", [P, 2, CH], F32R)
        g_lo = sb("g_lo", [P, 2, CH], F32R)
        hid = sb("e_hid", [P, AB, CH])
        gs = sb("gs", [P, 2, CH])
        z = sb("z", [P, 2, CH])
        yT = sb("yT", [P, CH])
        xf = sb("xf", [P, CH // P, D])

        p_hid = ps("e_phid", [P, HB, CH])
        p_eo = ps("p_eo", [P, 2, CH])
        p_g = ps("p_g", [P, 2, CH])
        p_y = ps("p_y", [P, CH])
        p_m = ps("p_m", [P, CH])

        zeroed = sem("e_zeroed")
        consts = sem("e_consts")
        w1_hi = sem("w1_hi")
        weights = sem("weights")
        xT_loaded = sem("e_xT_loaded")
        gT_loaded = sem("gT_loaded")
        xr_loaded = sem("e_xr_loaded")
        t_psum = sem("t_psum")
        t_ready = sem("t_ready")
        tr_hi = sem("tr_hi")
        tr_ready = sem("tr_ready")
        g_hi_ready = sem("g_hi_ready")
        g_split = sem("g_split")
        up_done = sem("up_done")
        gelu_done = sem("e_gelu_done")
        down_done = sem("down_done")
        g_psum = sem("g_psum")
        g_ready = sem("g_ready")
        z_ready = sem("z_ready")
        wo_done = sem("wo_done")
        yT_ready = sem("yT_ready")
        y_psum = sem("y_psum")
        xf_ready = sem("xf_ready")
        xf_stored = sem("xf_stored")

        N_CONST = 1 + PARTS + PARTS + 2 * PARTS + 2 + 2 + 1 + E // 2 + 1 + 1

        def over_chunks(eng, chunk):
            with eng.Fori(0, CHUNKS // 2 - 1) as i:
                chunk(2 * i, 0, False)
                chunk(2 * i + 1, 1, False)
            chunk(CHUNKS - 2, 0, False)
            chunk(CHUNKS - 1, 1, True)

        block = ctx.enter_context(nc.Block())

        @block.sync
        def _(sp):
            sp.sem_inc(xf_stored, 16)
            sp.dma_start(xT[:], xnT_dram[0]).then_inc(xT_loaded, 16)
            sp.dma_start(gT[:], gT_dram[0]).then_inc(gT_loaded, 16)
            sp.dma_start(ident[:], c["c_ident"]).then_inc(consts, 16)
            for part in range(PARTS):
                sp.dma_start(wm_rep[:, :, part, :], Wm.rearrange("k (s q) -> k s q", q=Q)).then_inc(consts, 16)
                sp.dma_start(bm_rep[part * Q:(part + 1) * Q, :], bm.rearrange("(s q) -> q s", q=Q),
                             allow_slow_non_contiguous=True)\
                    .then_inc(consts, 16)
            sp.wait_ge(zeroed, 1)
            for part in range(PARTS):
                for s in range(2):
                    r = part * Q + s * SD
                    sp.dma_start(w1f[r:r + SD, s, :].rearrange("d (e i) -> d e i", i=I),
                                 W1.rearrange("e d i -> d e i")).then_inc(consts, 16)
            sp.wait_ge(zeroed, 2)
            w2v = W2.rearrange("(ep two) i o -> two i ep o", two=2)
            b1v = b1.rearrange("(ep two) i -> two i ep", two=2)
            for e in range(2):
                sp.dma_start(w2p[e * I:(e + 1) * I, :, e * SD:(e + 1) * SD], w2v[e]).then_inc(consts, 16)
                sp.dma_start(b1c[e * I:(e + 1) * I, :], b1v[e], allow_slow_non_contiguous=True).then_inc(consts, 16)
            sp.dma_start(b2c[:], b2.rearrange("(h e) o -> (e o) h", h=2), allow_slow_non_contiguous=True).then_inc(consts, 16)
            for e in range(E // 2):
                sp.dma_start(wo_rep[e * SD:(e + 1) * SD, :, :], Wo.rearrange("(s o) n -> o s n", o=SD))\
                    .then_inc(consts, 16)
            sp.dma_start(boc[:], bo.rearrange("(n a) -> n a", a=1)).then_inc(consts, 16)
            sp.dma_start(self_[:], c["c_sel"].rearrange("p (u k) -> p u k", k=P)).then_inc(consts, 16)

            def chunk(n, par, last):
                if not last:
                    sp.wait_ge(t_psum, 4 * n + 4)
                    sp.dma_start(xT[:], xnT_dram[n + 1]).then_inc(xT_loaded, 16)
                    sp.wait_ge(g_split, n + 1)
                    sp.dma_start(gT[:], gT_dram[n + 1]).then_inc(gT_loaded, 16)
                sp.wait_ge(xf_ready, n + 1)
                sp.dma_start(xr[:], x.rearrange("(c k p) n -> c p k n", k=CH // P, p=P)[n]).then_inc(xr_loaded, 16)
                sp.wait_ge(xf_ready, n + 2)
                sp.dma_start(xf_dram.rearrange("(c k p) n -> c p k n", k=CH // P, p=P)[n], xf[:])\
                    .then_inc(xf_stored, 16)

            over_chunks(sp, chunk)
            sp.wait_ge(xf_stored, 16 * CHUNKS + 16)

        @block.gpsimd
        def _(pool):
            nc.gpsimd.memset(w1f[:], 0.0).then_inc(zeroed, 1)
            nc.gpsimd.memset(w2p[:], 0.0).then_inc(zeroed, 1)
            pool.wait_ge(consts, 16 * N_CONST)
            nc.gpsimd.tensor_copy(selr[:], self_[:]).then_inc(weights, 1)

        @block.scalar
        def _(act):
            act.sem_inc(gelu_done, HB)
            act.wait_ge(consts, 16 * N_CONST)

            def slots(n, k):
                act.wait_ge(tr_ready, 4 * n + k + 1)
                act.wait_ge(t_psum, 4 * n + k + 1)
                nc.scalar.activation(tt[:], p_m[:], ACT.Identity, bias=bm_rep[:, k:k + 1]).then_inc(t_ready, 1)

            for k in range(SP):
                slots(0, k)

            def chunk(n, par, last):
                for u in range(UNITS):
                    for q in range(EU):
                        j = EU * u + q
                        k = 64 * n + j
                        act.wait_ge(up_done, k + 1)
                        act.wait_ge(down_done, k + 1)
                        ep = (u % 2) * EU + q
                        nc.scalar.activation(hid[:, j % AB, :], p_hid[:, j % HB, :], ACT.Gelu,
                                             bias=b1c[:, ep:ep + 1]).then_inc(gelu_done, 1)
                    if not last and u % 2 == 0 and 2 <= u <= 8:
                        slots(n + 1, u // 2 - 1)

            over_chunks(act, chunk)

        @block.vector
        def _(dve):
            dve.sem_inc(tr_ready, 1)
            dve.sem_inc(g_ready, 2)
            dve.sem_inc(z_ready, 2)
            dve.sem_inc(yT_ready, 1)
            dve.sem_inc(xf_ready, 1)
            dve.wait_ge(consts, 16 * N_CONST)
            nc.vector.tensor_copy(w1r[:].rearrange("p s e i -> p s (e i)"), w1f[:]).then_inc(w1_hi, 1)
            dve.wait_ge(w1_hi, 1)
            for part in (1, 3):
                r = slice(part * Q, (part + 1) * Q)
                w = w1r[r].rearrange("p s e i -> p s (e i)")
                nc.vector.tensor_tensor(w, w1f[r], w.bitcast(F32), ALU.subtract).then_inc(weights, 1)

            def split_slots(n, par, k):
                if not isinstance(n, int) or n:
                    dve.wait_ge(up_done, 64 * n - 63)
                dve.wait_ge(t_ready, 4 * n + k + 1)
                nc.vector.tensor_copy(tr[:, par, k, :], tt[:]).then_inc(tr_hi, 1)
                dve.wait_ge(tr_hi, 4 * n + k + 1)
                low = tr[P // 2:, par, k, :]
                nc.vector.tensor_tensor(low, tt[P // 2:, :], low.bitcast(F32), ALU.subtract).then_inc(tr_ready, 1)

            def split_gates(n, par):
                if not isinstance(n, int) or n:
                    dve.wait_ge(g_psum, 16 * n - 15)
                dve.wait_ge(gT_loaded, 16 * n + 16)
                nc.vector.tensor_copy(g_hi[:, par, :], gT[:]).then_inc(g_hi_ready, 1)
                dve.wait_ge(g_hi_ready, n + 1)
                nc.vector.tensor_tensor(g_lo[:, par, :], gT[:], g_hi[:, par, :].bitcast(F32), ALU.subtract)\
                    .then_inc(g_split, 1)

            for k in range(SP):
                split_slots(0, 0, k)
            split_gates(0, 0)

            def chunk(n, par, last):
                for u in range(UNITS):
                    g = 16 * n + u
                    dve.wait_ge(g_psum, g + 1)
                    nc.vector.tensor_copy(gs[:, u % 2, :], p_g[:, u % 2, :]).then_inc(g_ready, 1)
                    dve.wait_ge(wo_done, g + 1)
                    dve.wait_ge(down_done, 4 * g + 4 + AB)
                    dve.wait_ge(g_ready, g + 1 + 2)
                    nc.vector.scalar_tensor_tensor(out=z[:, u % 2, :], in0=p_eo[:, u % 2, :],
                                                   scalar=b2c[:, u % 2:u % 2 + 1], in1=gs[:, u % 2, :],
                                                   op0=ALU.add, op1=ALU.mult).then_inc(z_ready, 1)
                    if not last and u % 2 == 0 and 2 <= u <= 8:
                        split_slots(n + 1, 1 - par, u // 2 - 1)
                    if not last and u == 10:
                        split_gates(n + 1, 1 - par)
                dve.wait_ge(wo_done, 16 * n + 16 + 2)
                dve.wait_ge(y_psum, n + 1)
                nc.vector.tensor_scalar(yT[:], p_y[:], boc[:], None, ALU.add).then_inc(yT_ready, 1)
                dve.wait_ge(xf_stored, 16 * n + 16)
                dve.wait_ge(xr_loaded, 16 * n + 16)
                dve.wait_ge(y_psum, n + 2)
                nc.vector.tensor_tensor(xf[:], p_m[:].rearrange("p (k n) -> p k n", n=D), xr[:], ALU.add)\
                    .then_inc(xf_ready, 1)

            over_chunks(dve, chunk)

        @block.tensor
        def _(pe):
            pe.sem_inc(down_done, AB)
            pe.sem_inc(wo_done, 2)
            pe.sem_inc(y_psum, 1)
            pe.wait_ge(consts, 16 * N_CONST)
            pe.wait_ge(weights, 3)

            def slots(n, k):
                if k:
                    pe.wait_ge(t_ready, 4 * n + k)
                elif not isinstance(n, int) or n:
                    pe.wait_ge(xf_ready, n)
                pe.wait_ge(xT_loaded, 16 * n + 16)
                nc.tensor.matmul(p_m[:], wm_rep[:, k].rearrange("p a q -> p (a q)"), xT[:],
                                 start=True, stop=True).then_inc(t_psum, 1)

            for k in range(SP):
                slots(0, k)

            def chunk(n, par, last):
                pe.wait_ge(g_split, n + 1)
                pe.wait_ge(tr_ready, 4 * n + 4 + 1)

                def down(j):
                    u, q = divmod(j, EU)
                    if q == 0:
                        pe.wait_ge(z_ready, 16 * n + u + 1)
                    pe.wait_ge(gelu_done, 64 * n + j + 1 + HB)
                    nc.tensor.matmul(p_eo[q * 2 * SD:(q + 1) * 2 * SD, u % 2, :], w2p[:, (u % 2) * EU + q, :],
                                     hid[:, j % AB, :], start=True, stop=True).then_inc(down_done, 1)

                def project(u):
                    if u == 0:
                        pe.wait_ge(yT_ready, n + 1)
                    pe.wait_ge(z_ready, 16 * n + u + 1 + 2)
                    nc.tensor.matmul(p_y[:], wo_rep[:, u // 2, :], z[:, u % 2, :],
                                     start=(u == 0), stop=(u == UNITS - 1)).then_inc(wo_done, 1)

                for u in range(UNITS):
                    s = u // 2
                    for q in range(EU):
                        j = EU * u + q
                        pe.wait_ge(gelu_done, 64 * n + j + 1)
                        nc.tensor.matmul(p_hid[:, j % HB, :], w1r[:, s % 2, (u % 2) * EU + q, :],
                                         tr[:, par, s // 2, :], start=True, stop=True).then_inc(up_done, 1)
                        if j >= 2:
                            down(j - 2)
                        if q == 1:
                            pe.wait_ge(g_ready, 16 * n + u + 1)
                            nc.tensor.matmul(p_g[:, u % 2, :], selr[:, u, :], g_hi[:, par, :], start=True, stop=False)
                            nc.tensor.matmul(p_g[:, u % 2, :], selr[:, u, :], g_lo[:, par, :], start=False, stop=True)\
                                .then_inc(g_psum, 1)
                        if q == 3 and u:
                            project(u - 1)
                    if not last and u % 2 == 0 and 2 <= u <= 8:
                        slots(n + 1, u // 2 - 1)
                down(EU * UNITS - 2)
                down(EU * UNITS - 1)
                project(UNITS - 1)
                if not last:
                    pe.wait_ge(t_ready, 4 * n + 8)
                pe.wait_ge(yT_ready, n + 2)
                for k in range(CH // P):
                    last_t = nc.tensor.transpose(p_m[:, k * P:(k + 1) * P], yT[:, k * P:(k + 1) * P], ident[:])
                last_t.then_inc(y_psum, 1)

            over_chunks(pe, chunk)


def attention(nc, w_qkv, w_o, log_p, log_a, w1, b1, w2, b2, c, xnT_dram, xf_dram, out):
    with ExitStack() as ctx:
        def sb(name, shape, dt=F32):
            return ctx.enter_context(nc.sbuf_tensor(name, shape, dt))

        def ps(name, shape):
            return ctx.enter_context(nc.psum_tensor(name, shape, F32))

        def sem(name):
            return ctx.enter_context(nc.semaphore(name))

        HC = HALF * C
        HH = HALF * H

        ident = sb("a_ident", [P, P])
        wqkv = sb("wqkv", [D, 3 * H * HD])
        wo = sb("wo", [P, PAIRS, D])
        w_up = sb("w_up", [P, 2, HC])
        w_down = sb("w_down", [HC, HH])
        cols = sb("cols", [P, 12])
        cos = sb("cos", [P, L])
        sin = sb("sin", [P, L])
        ker_mask = sb("ker_mask", [P, L])
        xa = sb("xa", [P, 2, RING, L])
        std = sb("std", [P, H, L])
        hid = sb("hid", [P, HIDS, 2, L])
        pr = sb("pr", [P, TILES, L])
        pT = sb("pT", [P, QB, H, GQ])
        vv = sb("vv", [P, QB, H * HD])
        kk = sb("kk", [P, PAIRS, L])
        raw = sb("raw", [P, 2, PAIRS, P])
        rot = sb("rot", [P, 2, PAIRS, P])
        q = sb("q", [P, PAIRS, P])
        xT = sb("a_xT", [P, QB, P])
        oT = sb("oT", [P, PAIRS, P])
        xf = sb("a_xf", [P, D])
        y = sb("y", [P, D])
        mx = sb("mx", [P, TILES])
        nmx = sb("nmx", [P, TILES])
        sums = sb("sums", [P, TILES])
        rsum = sb("rsum", [P, TILES])
        dist = std[:, 0, :]
        mask = std[:, 1, :]
        ker = std[:, 2, :]

        p_up = ps("p_up", [P, 2, 2, L])
        p_down = ps("p_down", [P, 2, L])
        p_gap = ps("p_gap", [P, 2, L])

        zeroed = sem("a_zeroed")
        consts = sem("a_consts")
        pr_zeroed = sem("pr_zeroed")
        sp_abs = sem("sp_abs")
        sp_exp = sem("sp_exp")
        sp_ln = sem("sp_ln")
        sp_sum = sem("sp_sum")
        ker_ln = sem("ker_ln")
        ker_ready = sem("ker_ready")
        tables = sem("tables")
        ker_placed = sem("ker_placed")
        xT_loaded = [sem(f"xT_loaded{i}") for i in range(QB)]
        xf_loaded = sem("a_xf_loaded")
        rot_loaded = sem("rot_loaded")
        ropeq = sem("ropeq")
        ropek = sem("ropek")
        qstep = sem("qstep")
        kstep = sem("kstep")
        x_loaded = [sem(f"a_x_loaded{i}") for i in range(RING)]
        up_done = sem("a_up_done")
        gelu_done = sem("a_gelu_done")
        down_done = sem("a_down_done")
        sc_ready = sem("sc_ready")
        logit_turn = sem("logit_turn")
        norm_turn = sem("norm_turn")
        load_turn = sem("load_turn")
        pool_turn = sem("pool_turn")
        logit_done = sem("logit_done")
        nmx_ready = sem("nmx_ready")
        exp_done = sem("exp_done")
        rsum_ready = sem("rsum_ready")
        norm_done = sem("norm_done")
        gap_fill = sem("gap_fill")
        gap_read = sem("gap_read")
        y_stored = sem("y_stored")

        N_CONST = 7 + 2 * 2 * HALF + HALF + HALF + 3 * TQ
        PROLOGUE = 4 + H + 4

        def plan(last_batch):
            at, base = {}, 0
            for ib in range(QB):
                more = last_batch and ib == QB - 1
                more2 = last_batch and ib >= QB - 2
                for kind, count in (("v", 2), ("qk", 0 if more2 else 4), ("t0", 2 * (ib + 1)), ("pv0", 1),
                                    ("scores", 0 if more else H), ("t1", 2 * (ib + 1)), ("pv1", 1), ("o", 1)):
                    at[ib, kind] = base
                    base += count
            return at, base

        UNITS, PER_BATCH = plan(False)
        UNITS_LAST, _ = plan(True)

        def unit(b, ib, kind, k=0):
            at = (UNITS_LAST if isinstance(b, int) else UNITS)[ib, kind] + k
            return PER_BATCH * b + (PROLOGUE + at), at % 2

        assert PER_BATCH % 2 == 0 and PROLOGUE % 2 == 0

        def over_batches(eng, step):
            with eng.Fori(0, B - 1) as b:
                for ib in range(QB):
                    step(b, ib, False)
            for ib in range(QB):
                step(B - 1, ib, True)

        def ahead(b, ib, m):
            return (b, ib + m) if ib + m < QB else (b + 1, ib + m - QB)

        def window(t):
            return slice(L - TQ * (t + 1), L)

        def keys(ib, t):
            return slice(L - (ib + 1) * P, L - P + TQ * (t + 1))

        def tiled(a, apart):
            v = a.rearrange("p c (a n) -> p (c a) n", n=4 * TQ)
            return v.rearrange("p a (i b) -> p a b i", b=4) if apart else v.rearrange("p a (b i) -> p a b i", b=4)

        def fillers(ib, r):
            n = 2 * (ib + 1)
            return [u for u in range(n) if 1 + u * (GT - 2) // n == r]

        def wide(table):
            return table.unsqueeze(1).broadcast_to([P, PAIRS, P])

        block = ctx.enter_context(nc.Block())

        @block.sync
        def _(sp):
            sp.dma_start(wqkv[:], w_qkv).then_inc(consts, 16)
            sp.dma_start(xT[:, 0, :], xnT_dram[0, :, 0:P]).then_inc(xT_loaded[0], 16)
            sp.dma_start(xT[:, 1, :], xnT_dram[0, :, P:2 * P]).then_inc(xT_loaded[1], 16)
            sp.dma_start(cos[:], c["c_cos"]).then_inc(consts, 16)
            sp.dma_start(sin[:], c["c_sin"]).then_inc(consts, 16)
            sp.dma_start(dist, c["c_dist"]).then_inc(consts, 16)
            sp.dma_start(mask, c["c_mask"]).then_inc(consts, 16)
            sp.dma_start(ident[:], c["c_ident"]).then_inc(consts, 16)
            for i in range(TQ):
                r = slice(i * H, (i + 1) * H)
                sp.dma_start(cols[r, 0:1], log_p).then_inc(consts, 16)
                sp.dma_start(cols[r, 1:2], log_a).then_inc(consts, 16)
                sp.dma_start(cols[r, 2:3], b2.rearrange("(n a) -> n a", a=1)).then_inc(consts, 16)
            sp.wait_ge(zeroed, 1)
            for i in range(HALF):
                sp.dma_start(cols[i * C:(i + 1) * C, 3:4], b1.rearrange("(n a) -> n a", a=1)).then_inc(consts, 16)
                sp.dma_start(w_down[i * C:(i + 1) * C, i * H:(i + 1) * H], w2).then_inc(consts, 16)
                for half in range(2):
                    for kind in range(2):
                        r = HH * (half ^ kind) + i * H
                        sp.dma_start(w_up[r:r + H, half, i * C:(i + 1) * C], w1[kind * H:(kind + 1) * H, :])\
                            .then_inc(consts, 16)
            sp.dma_start(wo[:], w_o.rearrange("(c k) n -> k c n", k=P)).then_inc(consts, 16)
            sp.wait_ge(ker_ready, 1)
            for r in range(RING):
                sp.dma_start(xa[HH:, 0, r, :], ker[:HH, :]).then_inc(ker_placed, 16)
                sp.dma_start(xa[:HH, 1, r, :], ker[HH:, :]).then_inc(ker_placed, 16)
            sp.wait_ge(ker_placed, 16 * 2 * RING)

            def rotate():
                for h in range(4):
                    to, fr = h * 32, (h ^ 1) * 32
                    sp.dma_start(rot[to:to + 32], raw[fr:fr + 32]).then_inc(rot_loaded, 16)

            def load(b, ib, t):
                g = 64 * b + (16 * ib + t)
                n_keys = TQ * (16 * ib + t + 1)
                row = 32 * (t // 4) + t % 4
                sp.wait_ge(up_done, g + 1)
                sp.wait_ge(sc_ready, g + 1)
                for half in range(2):
                    fr = row + 16 * half
                    sp.dma_start(xa[HH * half:HH * half + HH, half, t % RING, window(16 * ib + t)],
                                 std[fr:fr + 13:4, :, 0:n_keys]).then_inc(x_loaded[t % RING], 16)

            sp.sem_inc(y_stored, 16)
            sp.wait_ge(gap_read, 4 + 2)
            rotate()
            sp.wait_ge(gap_read, 4 + H + 2)
            for t in range(RING):
                load(0, 0, t)
            sp.wait_ge(gap_read, PROLOGUE + 2)

            out_rows = out.rearrange("(b k p) n -> b k p n", k=QB, p=P)
            xf_rows = xf_dram.rearrange("(b k p) n -> b k p n", k=QB, p=P)

            def step(b, ib, last):
                more = not (last and ib == QB - 1)
                if more:
                    rotate()
                if not (last and ib >= QB - 2):
                    bn, ibn = ahead(b, ib, 2)
                    sp.dma_start(xT[:, ibn, :], xnT_dram[bn, :, ibn * P:(ibn + 1) * P]).then_inc(xT_loaded[ibn], 16)
                sp.dma_start(xf[:], xf_rows[b, ib]).then_inc(xf_loaded, 16)
                for t in range(RING, TILES):
                    load(b, ib, t)
                if more:
                    sp.wait_ge(gap_read, unit(b, ib, "scores", H)[0] + 2)
                    sp.sem_inc(load_turn, 1)
                    for t in range(RING):
                        load(*ahead(b, ib, 1), t)
                sp.wait_ge(gap_read, unit(b, ib, "o")[0] + 1 + 2)
                sp.dma_start(out_rows[b, ib], y[:]).then_inc(y_stored, 16)

            over_batches(sp, step)
            sp.wait_ge(y_stored, 16 * BLOCKS + 16)

        @block.gpsimd
        def _(pool):
            nc.gpsimd.memset(w_up[:], 0.0)
            nc.gpsimd.memset(w_down[:], 0.0).then_inc(zeroed, 1)
            nc.gpsimd.memset(pr[:], 0.0).then_inc(pr_zeroed, 1)
            pool.sem_inc(sc_ready, RING)
            pool.wait_ge(pr_zeroed, 1)
            pool.wait_ge(tables, 1)

            def rope_keys(b, ib):
                m = 4 * b + ib
                cs = slice(ib * P, (ib + 1) * P)
                pool.wait_ge(rot_loaded, 64 * m + 64)
                nc.gpsimd.tensor_tensor(raw[:, 1], raw[:, 1], wide(cos[:, cs]), ALU.mult).then_inc(kstep, 1)
                nc.gpsimd.tensor_tensor(rot[:, 1], rot[:, 1], wide(sin[:, cs]), ALU.mult).then_inc(kstep, 1)
                pool.wait_ge(kstep, 2 * m + 2)
                nc.gpsimd.tensor_tensor(kk[:, :, cs], raw[:, 1], rot[:, 1], ALU.add).then_inc(ropek, 1)

            rope_keys(0, 0)
            pool.wait_ge(ropek, 1)

            def step(b, ib, last):
                for t in range(TILES):
                    w, wx = keys(ib, t), window(16 * ib + t)
                    pool.wait_ge(x_loaded[t % RING], 32 * (8 * b + (2 * ib + t // RING)) + 32)
                    for half in range(2):
                        r = slice(HH * half, HH * half + HH)
                        last_add = nc.gpsimd.tensor_tensor(pr[r, t, w], xa[r, half, t % RING, wx], ker_mask[r, wx],
                                                           ALU.add)
                    last_add.then_inc(sc_ready, 1)
                    if t == 7 and not (last and ib == QB - 1):
                        pool.wait_ge(sc_ready, 64 * b + (16 * ib + t + 1) + RING)
                        pool.sem_inc(pool_turn, 1)
                        rope_keys(*ahead(b, ib, 1))
                        pool.wait_ge(ropek, 4 * b + (ib + 2))
                        pool.sem_inc(pool_turn, 1)

            over_batches(pool, step)

        @block.scalar
        def _(act):
            act.sem_inc(gelu_done, 2)
            act.wait_ge(consts, 16 * N_CONST)
            act.wait_ge(sp_abs, 1)
            nc.scalar.activation(cols[:, 6:8], cols[:, 4:6], ACT.Exp, scale=-1.0).then_inc(sp_exp, 1)
            act.wait_ge(sp_exp, 1)
            nc.scalar.activation(cols[:, 8:10], cols[:, 6:8], ACT.Ln, bias=1.0).then_inc(sp_ln, 1)
            act.wait_ge(sp_sum, 1)
            nc.scalar.activation(ker, dist, ACT.Ln, bias=1.0, scale=cols[:, 11:12]).then_inc(ker_ln, 1)

            def step(b, ib, last):
                for G in range(GROUPS):
                    for t in range(GT * G, GT * G + GT):
                        g = 64 * b + (16 * ib + t)
                        n_keys = TQ * (16 * ib + t + 1)
                        act.wait_ge(down_done, 64 * b + (16 * ib + (t + 1 if t >= HIDS else HIDS)))
                        act.wait_ge(up_done, g + 1 + RING)
                        nc.scalar.activation(hid[:, t % HIDS, :, 0:n_keys], p_up[:, t % 2, :, 0:n_keys], ACT.Gelu,
                                             bias=cols[:, 3:4]).then_inc(gelu_done, 1)
                    act.wait_ge(nmx_ready, 8 * b + (2 * ib + G) + 1)
                    for t in range(GT * G, GT * G + GT):
                        nc.scalar.activation(pr[:, t, keys(ib, t)], pr[:, t, keys(ib, t)], ACT.Exp,
                                             bias=nmx[:, t:t + 1], accum_out=sums[:, t:t + 1]).then_inc(exp_done, 1)

            over_batches(act, step)

        @block.vector
        def _(dve):
            dve.sem_inc(logit_done, 2)
            dve.sem_inc(gap_read, 2)
            dve.wait_ge(consts, 16 * N_CONST)
            nc.vector.scalar_tensor_tensor(out=cols[:, 4:6], in0=cols[:, 0:2], scalar=-1.0, in1=cols[:, 0:2],
                                           op0=ALU.mult, op1=ALU.max).then_inc(sp_abs, 1)
            dve.wait_ge(sp_ln, 1)
            nc.vector.scalar_tensor_tensor(out=cols[:, 10:12], in0=cols[:, 0:2], scalar=0.0, in1=cols[:, 8:10],
                                           op0=ALU.max, op1=ALU.add).then_inc(sp_sum, 1)
            dve.wait_ge(ker_ln, 1)
            nc.vector.tensor_scalar(ker, ker, cols[:, 10:11], -1.0, ALU.mult, ALU.mult).then_inc(ker_ready, 1)
            dve.wait_ge(ker_ready, 1)
            nc.vector.scalar_tensor_tensor(out=ker_mask[:], in0=ker, scalar=cols[:, 2:3], in1=mask,
                                           op0=ALU.add, op1=ALU.add).then_inc(tables, 1)

            dve.wait_ge(pr_zeroed, 1)

            def scores_read(at, ib, after=lambda h: None):
                w = slice(0, (ib + 1) * P)
                for h in range(H):
                    k, bank = at(h)
                    dve.wait_ge(gap_fill, k + 1)
                    nc.vector.tensor_scalar(std[:, h, w], p_gap[:, bank, w], HD ** -0.5, None, ALU.mult)\
                        .then_inc(gap_read, 1)
                    after(h)

            def qk_read(at, m):
                for j in range(4):
                    k, bank = at(j)
                    if j == 2 and (not isinstance(m, int) or m):
                        dve.wait_ge(ropek, m)
                    dve.wait_ge(gap_fill, k + 1)
                    nc.vector.tensor_copy(raw[:, j // 2, (j % 2) * 4:(j % 2) * 4 + 4, :],
                                          p_gap[:, bank, :].rearrange("p (c n) -> p c n", n=P)).then_inc(gap_read, 1)

            def rope_queries(b, ib):
                m = 4 * b + ib
                cs = slice(ib * P, (ib + 1) * P)
                dve.wait_ge(rot_loaded, 64 * m + 64)
                nc.vector.tensor_tensor(raw[:, 0], raw[:, 0], wide(cos[:, cs]), ALU.mult).then_inc(qstep, 1)
                nc.vector.tensor_tensor(rot[:, 0], rot[:, 0], wide(sin[:, cs]), ALU.mult).then_inc(qstep, 1)
                dve.wait_ge(qstep, 2 * m + 2)
                nc.vector.tensor_tensor(tiled(q[:], True), tiled(raw[:, 0], False), tiled(rot[:, 0], False), ALU.add)\
                    .then_inc(ropeq, 1)

            qk_read(lambda j: (j, j % 2), 0)
            rope_queries(0, 0)
            dve.wait_ge(ker_placed, 16 * 2 * RING)
            dve.wait_ge(tables, 1)
            scores_read(lambda j: (4 + j, j % 2), 0)
            qk_read(lambda j: (4 + H + j, j % 2), 1)

            def step(b, ib, last):
                more = not (last and ib == QB - 1)

                def logits(t):
                    g = 64 * b + (16 * ib + t)
                    n_keys = TQ * (16 * ib + t + 1)
                    w = keys(ib, t)
                    dve.wait_ge(down_done, g + 1 + HIDS)
                    dve.wait_ge(sc_ready, g + 1 + RING)
                    dve.sem_inc(logit_turn, 1)
                    nc.vector.tensor_tensor_reduce(
                        out=pr[:, t, w], in0=p_down[:, t % 2, 0:n_keys], in1=pr[:, t, w],
                        scale=1.0, scalar=-3e38, op0=ALU.add, op1=ALU.max, accum_out=mx[:, t:t + 1])\
                        .then_inc(logit_done, 1)

                def negate_maxima(G):
                    r = slice(GT * G, GT * G + GT)
                    dve.wait_ge(logit_done, 64 * b + (16 * ib + GT * G + GT) + 2)
                    nc.vector.tensor_scalar(nmx[:, r], mx[:, r], -1.0, None, ALU.mult).then_inc(nmx_ready, 1)

                def inverse_sums(j):
                    dve.wait_ge(exp_done, 64 * b + (16 * ib + 4 * j + 4))
                    nc.vector.reciprocal(rsum[:, 4 * j:4 * j + 4], sums[:, 4 * j:4 * j + 4]).then_inc(rsum_ready, 1)

                def normalise(j):
                    dve.wait_ge(rsum_ready, 16 * b + (4 * ib + j) + 1)
                    dve.sem_inc(norm_turn, 1)
                    for t in range(4 * j, 4 * j + 4):
                        nc.vector.tensor_scalar(pr[:, t, keys(ib, t)], pr[:, t, keys(ib, t)], rsum[:, t:t + 1], None,
                                                ALU.mult).then_inc(norm_done, 1)

                def transposed(G, u):
                    four, kb = divmod(u, ib + 1)
                    k, bank = unit(b, ib, f"t{G}", u)
                    dve.wait_ge(gap_fill, k + 1)
                    nc.vector.tensor_copy(pT[:, kb, :, 4 * TQ * four:4 * TQ * (four + 1)],
                                          p_gap[:, bank, :].rearrange("p (i h) -> p h i", h=H)).then_inc(gap_read, 1)

                def values(G):
                    k, bank = unit(b, ib, f"pv{G}")
                    dve.wait_ge(gap_fill, k + 1)
                    nc.vector.tensor_copy(oT[:, :, GQ * G:GQ * G + GQ],
                                          p_gap[:, bank, :].rearrange("p (c n) -> p c n", n=GQ)).then_inc(gap_read, 1)

                for t in range(GT):
                    logits(t)
                    if t == 5 and more:
                        rope_queries(*ahead(b, ib, 1))
                negate_maxima(0)
                for j in range(2):
                    k, bank = unit(b, ib, "v", j)
                    dve.wait_ge(gap_fill, k + 1)
                    nc.vector.tensor_copy(vv[:, ib, j * L:(j + 1) * L], p_gap[:, bank, :]).then_inc(gap_read, 1)
                if not (last and ib >= QB - 2):
                    qk_read(lambda j: unit(b, ib, "qk", j), 4 * b + (ib + 2))
                for j in range(2):
                    inverse_sums(j)
                for j in range(2):
                    normalise(j)
                for r in range(GT):
                    if r >= LAG:
                        logits(GT + r - LAG)
                    for u in fillers(ib, r):
                        transposed(0, u)
                values(0)
                logits(TILES - 2)
                if more:
                    def between(h):
                        if h == 1:
                            logits(TILES - 1)
                            negate_maxima(1)
                        if h in (7, 11):
                            inverse_sums(2 + (h == 11))
                        if h in (8, 12):
                            normalise(2 + (h == 12))

                    scores_read(lambda j: unit(b, ib, "scores", j), (ib + 1) % QB, between)
                else:
                    logits(TILES - 1)
                    negate_maxima(1)
                    for j in range(2, 4):
                        inverse_sums(j)
                        normalise(j)
                for u in range(2 * (ib + 1)):
                    transposed(1, u)
                values(1)
                n = 4 * b + ib
                k, bank = unit(b, ib, "o")
                dve.wait_ge(y_stored, 16 * n + 16)
                dve.wait_ge(xf_loaded, 16 * n + 16)
                dve.wait_ge(gap_fill, k + 1)
                nc.vector.tensor_tensor(y[:], p_gap[:, bank, 0:D], xf[:], ALU.add).then_inc(gap_read, 1)

            over_batches(dve, step)

        @block.tensor
        def _(pe):
            pe.sem_inc(up_done, RING)
            pe.sem_inc(down_done, HIDS)
            pe.wait_ge(consts, 16 * N_CONST)

            def qk_unit(at, j, b, ib):
                k, bank = at(j)
                if j == 0:
                    pe.wait_ge(xT_loaded[ib], 16 * b + 16)
                pe.wait_ge(gap_read, k + 1)
                for i in range(4):
                    m = 4 * j + i
                    last_mm = nc.tensor.matmul(p_gap[:, bank, i * P:(i + 1) * P], wqkv[:, m * P:(m + 1) * P],
                                               xT[:, ib, :], start=True, stop=True)
                last_mm.then_inc(gap_fill, 1)

            def scores_unit(at, h, b, ib):
                k, bank = at(h)
                if h == 0:
                    pe.wait_ge(ropeq, 4 * b + ib + 1)
                    pe.wait_ge(ropek, 4 * b + ib + 1)
                r = slice(HD * (h % 2), HD * (h % 2) + HD)
                n_keys = (ib + 1) * P
                pe.wait_ge(gap_read, k + 1)
                nc.tensor.matmul(p_gap[:, bank, 0:n_keys],
                                 q[r, h // 2, :], kk[r, h // 2, 0:n_keys], start=True, stop=True).then_inc(gap_fill, 1)

            for j in range(4):
                qk_unit(lambda j: (j, j % 2), j, 0, 0)
            for h in range(H):
                scores_unit(lambda j: (4 + j, j % 2), h, 0, 0)
            for j in range(4):
                qk_unit(lambda j: (4 + H + j, j % 2), j, 0, 1)
            pe.wait_ge(ker_placed, 16 * 2 * RING)

            def step(b, ib, last):
                more = not (last and ib == QB - 1)

                def up(t):
                    g = 64 * b + (16 * ib + t)
                    n_keys = TQ * (16 * ib + t + 1)
                    pe.wait_ge(x_loaded[t % RING], 32 * (8 * b + (2 * ib + t // RING)) + 32)
                    pe.wait_ge(gelu_done, g + 1)
                    for half in range(2):
                        last_mm = nc.tensor.matmul(p_up[:, t % 2, half, 0:n_keys], w_up[:, half, :],
                                                   xa[:, half, t % RING, window(16 * ib + t)], start=True, stop=True)
                    last_mm.then_inc(up_done, 1)

                def down(t):
                    g = 64 * b + (16 * ib + t)
                    n_keys = TQ * (16 * ib + t + 1)
                    pe.wait_ge(logit_done, g + 1)
                    pe.wait_ge(gelu_done, g + 1 + 2)
                    for half in range(2):
                        last_mm = nc.tensor.matmul(p_down[HH * half:HH * half + HH, t % 2, 0:n_keys], w_down[:],
                                                   hid[:, t % HIDS, half, 0:n_keys], start=True, stop=True)
                    last_mm.then_inc(down_done, 1)

                def v_unit(j):
                    k, bank = unit(b, ib, "v", j)
                    pe.wait_ge(gap_read, k + 1)
                    v0 = 2 * H * HD + j * L
                    nc.tensor.matmul(p_gap[:, bank, :], xT[:, ib, :], wqkv[:, v0:v0 + L], start=True, stop=True)\
                        .then_inc(gap_fill, 1)

                def transpose(G, u):
                    four, kb = divmod(u, ib + 1)
                    k, bank = unit(b, ib, f"t{G}", u)
                    if kb == 0:
                        pe.wait_ge(norm_done, 64 * b + (16 * ib + GT * G + 4 * four + 4))
                    pe.wait_ge(gap_read, k + 1)
                    c0 = L - (ib + 1 - kb) * P
                    for i in range(4):
                        last_mm = nc.tensor.transpose(p_gap[:, bank, i * P:(i + 1) * P],
                                                      pr[:, GT * G + 4 * four + i, c0:c0 + P], ident[:])
                    last_mm.then_inc(gap_fill, 1)

                def values(G):
                    k, bank = unit(b, ib, f"pv{G}")
                    pe.wait_ge(gap_read, k + 2)
                    for i in range(PAIRS):
                        for kb in range(ib + 1):
                            for r in range(2):
                                h = 2 * i + r
                                last_mm = nc.tensor.matmul(
                                    p_gap[HD * r:HD * r + HD, bank, i * GQ:(i + 1) * GQ],
                                    vv[:, kb, h * HD:(h + 1) * HD], pT[:, kb, h, :],
                                    start=(kb == 0), stop=(kb == ib))
                    last_mm.then_inc(gap_fill, 1)

                for t in range(GT):
                    up(t)
                    if t >= LAG:
                        down(t - LAG)
                down(GT - 2)
                down(GT - 1)
                for j in range(2):
                    v_unit(j)
                if not (last and ib >= QB - 2):
                    for j in range(4):
                        qk_unit(lambda j: unit(b, ib, "qk", j), j, *ahead(b, ib, 2))
                for r in range(GT):
                    up(GT + r)
                    if r >= LAG:
                        down(GT + r - LAG)
                    for u in fillers(ib, r):
                        transpose(0, u)
                values(0)
                down(TILES - 2)
                for h in range(H if more else 0):
                    scores_unit(lambda j: unit(b, ib, "scores", j), h, *ahead(b, ib, 1))
                    if h == 1:
                        down(TILES - 1)
                if not more:
                    down(TILES - 1)
                for u in range(2 * (ib + 1)):
                    transpose(1, u)
                values(1)
                k, bank = unit(b, ib, "o")
                pe.wait_ge(gap_read, k + 2)
                for i in range(PAIRS):
                    last_mm = nc.tensor.matmul(p_gap[:, bank, 0:D], oT[:, i, :], wo[:, i, :],
                                               start=(i == 0), stop=(i == PAIRS - 1))
                last_mm.then_inc(gap_fill, 1)

            over_batches(pe, step)


def build(nc, a, c, out):
    xnT_dram = nc.dram_tensor("xnT_scratch", [CHUNKS, D, CH], F32, kind="Internal").ap()
    gT_dram = nc.dram_tensor("gT_scratch", [CHUNKS, P, CH], F32, kind="Internal").ap()
    xf_dram = nc.dram_tensor("xf_scratch", [ROWS, D], F32, kind="Internal").ap()
    x = a["L0_attn_x"].rearrange("b l d -> (b l) d")
    heads = lambda v: v.rearrange("h a b -> h (a b)")
    norm_and_gates(nc, x, a["L0_ffn_Wm"], a["L0_ffn_bm"], a["L0_ffn_expert_emb"], c, xnT_dram, gT_dram)
    experts(nc, x, a["L0_ffn_Wm"], a["L0_ffn_bm"], a["L0_ffn_W1"], a["L0_ffn_b1"], a["L0_ffn_W2"], a["L0_ffn_b2"],
            a["L0_ffn_Wo"], a["L0_ffn_bo"], c, xnT_dram, gT_dram, xf_dram)
    attention(nc, a["L0_attn_w_qkv"], a["L0_attn_w_o"], heads(a["L0_attn_log_p"]), heads(a["L0_attn_log_a"]),
              a["L0_attn_w1"], a["L0_attn_b1"], a["L0_attn_w2"], a["L0_attn_b2"], c, xnT_dram, xf_dram,
              out.rearrange("b l d -> (b l) d"))


_INS = ["L0_attn_x", "L0_attn_w_qkv", "L0_attn_w_o", "L0_attn_log_p", "L0_attn_log_a", "L0_attn_w1", "L0_attn_b1",
        "L0_attn_w2", "L0_attn_b2", "L0_ffn_Wm", "L0_ffn_bm", "L0_ffn_expert_emb", "L0_ffn_W1", "L0_ffn_b1",
        "L0_ffn_W2", "L0_ffn_b2", "L0_ffn_Wo", "L0_ffn_bo"]


def kernel(**inputs):
    import numpy as _np
    import concourse.bacc as _bacc
    from concourse import mybir as _mybir
    from concourse.bass_utils import run_bass_kernel_spmd as _run

    nc = _bacc.Bacc("TRN2", target_bir_lowering=False, num_devices=1)
    arrays, args, consts = {}, {}, {}
    for name in _INS:
        a = _np.ascontiguousarray(inputs[name])
        arrays[f"in_{name}"] = a
        args[name] = nc.dram_tensor(f"in_{name}", a.shape, _mybir.dt.from_np(a.dtype), kind="ExternalInput").ap()
    for name, a in shape_constants().items():
        a = _np.ascontiguousarray(a)
        arrays[name] = a
        consts[name] = nc.dram_tensor(name, a.shape, _mybir.dt.from_np(a.dtype), kind="ExternalInput").ap()
    out = nc.dram_tensor("out_0", (B, L, D), _mybir.dt.float32, kind="ExternalOutput").ap()
    build(nc, args, consts, out)
    r = _run(nc, [arrays], core_ids=[0])
    return r.results[0]["out_0"]
```

```python
from contextlib import ExitStack

import numpy as np

import concourse.bass as bass
from concourse import mybir

F32 = mybir.dt.float32
F32R = mybir.dt.float32r
ALU = mybir.AluOpType
ACT = mybir.ActivationFunctionType
AX = mybir.AxisListType.X

P = 128
B, L, D = 8, 512, 128
ROWS = B * L
BLOCKS = ROWS // P
H, HD = 16, 64
C = 2 * H
PAIRS = H // 2
QB = L // P
TQ = 8
TILES = P // TQ
HALF = TQ // 2
GT = 8
RING = 4
GROUPS = TILES // GT
GQ = GT * TQ
SCORES_BESIDE = (6, 6, 2, 2, 0, 0, 0, 0)
ROPE_BESIDE = (5, 6, 7)
LAG = 2
HIDS = 2
S, SD = 8, 16
E, I = 16, 64
EP = E // 2
CH = 512
CHUNKS = ROWS // CH
EPS = 1e-5
MASKED = -1e30


def shape_constants():
    f = np.float32
    inv_freq = (f(1.0) / np.power(f(10000.0), np.arange(0, HD, 2, dtype=f) / f(HD))).astype(f)
    freqs = np.outer(np.arange(L, dtype=f), inv_freq).astype(f)
    emb = np.concatenate([freqs, freqs], -1)
    cos, sin = np.cos(emb).astype(f).T, np.sin(emb).astype(f).T
    sign = np.where(np.arange(HD) < HD // 2, f(-1), f(1))[:, None]
    cols = np.arange(L) - (L - TQ)
    dist = (np.arange(P) // H)[:, None] - cols[None]
    e_rev = np.broadcast_to((E - np.arange(E)).astype(f), (P, BLOCKS * S, E))
    k = np.arange(P)
    sel = np.zeros((P, S, 2, P), f)
    for s in range(S):
        for half in range(2):
            want = s * E + half * (E // 2) + k // SD
            sel[want, s, half, k] = 1
    return {
        "c_ident": np.eye(P, dtype=f),
        "c_cos": np.concatenate([cos, cos]),
        "c_sin": np.concatenate([sin * sign, sin * sign]),
        "c_dist": np.abs(dist).astype(f),
        "c_mask": np.where(dist < 0, f(MASKED), f(0)),
        "c_erev": np.ascontiguousarray(e_rev[:, 0]),
        "c_sel": sel.reshape(P, S * 2 * P),
    }


def norm_and_gates(nc, x, Wm, bm, emb, c, xnT_dram, gT_dram):
    with ExitStack() as ctx:
        def sb(name, shape, dt=F32):
            return ctx.enter_context(nc.sbuf_tensor(name, shape, dt))

        def ps(name, shape):
            return ctx.enter_context(nc.psum_tensor(name, shape, F32))

        def sem(name):
            return ctx.enter_context(nc.semaphore(name))

        G = 4 * S
        x_all = sb("x_all", [P, BLOCKS, D])
        ident = sb("n_ident", [P, P])
        wm = sb("n_wm", [D, D])
        bmc = sb("n_bmc", [D, 1])
        emb_bd = sb("emb_bd", [P, P])
        erev = sb("erev", [P, E])
        stats = sb("stats", [P, BLOCKS, 6])
        small = sb("n_small", [P, 5, BLOCKS])
        xn = sb("xn", [P, 4, P])
        xT = sb("n_xT", [P, CH])
        hT = sb("n_hT", [P, CH])
        logit = sb("logit", [P, G, E])
        ex = sb("ex", [P, G, E])
        prob = sb("n_prob", [P, G, E])
        gate = sb("n_gate", [P, G, E])
        t1 = sb("t1", [P, G, E])
        first = sb("first", [P, G, E])
        red = sb("red", [P, 6, G])
        gT = sb("n_gT", [P, CH])
        pT = ps("n_pT", [P, CH])
        pH = ps("n_pH", [P, CH])
        pL = ps("n_pL", [P, CH])
        pG = ps("n_pG", [P, CH])

        zeroed = sem("n_zeroed")
        consts = sem("n_consts")
        QUARTERS = 4
        KQ = BLOCKS // QUARTERS
        x_loaded = [sem(f"x_loaded{j}") for j in range(QUARTERS)]
        step = sem("n_step")
        var_ready = sem("var_ready")
        std_ready = sem("std_ready")
        xn_ready = sem("xn_ready")
        xT_psum = sem("xT_psum")
        xT_ready = sem("xT_ready")
        xT_stored = sem("xT_stored")
        hT_psum = sem("hT_psum")
        hT_ready = sem("hT_ready")
        lg_psum = sem("lg_psum")
        diff_ready = sem("diff_ready")
        ex_ready = sem("ex_ready")
        rinv_ready = sem("rinv_ready")
        prob_ready = sem("n_prob_ready")
        gates_ready = sem("gates_ready")
        gT_psum = sem("gT_psum")
        gT_ready = sem("gT_ready")
        gT_stored = sem("gT_stored")

        N_CONST = 4 + S
        bc = lambda a: a.unsqueeze(2).broadcast_to([P, G, E])

        block = ctx.enter_context(nc.Block())

        @block.sync
        def _(sp):
            sp.sem_inc(xT_stored, 16)
            sp.sem_inc(gT_stored, 16)
            for j in range(QUARTERS):
                sp.dma_start(x_all[:, KQ * j:KQ * (j + 1), :], x.rearrange("(k p) n -> p k n", p=P)
                             [:, KQ * j:KQ * (j + 1), :]).then_inc(x_loaded[j], 16)
            sp.dma_start(ident[:], c["c_ident"]).then_inc(consts, 16)
            sp.dma_start(wm[:], Wm).then_inc(consts, 16)
            sp.dma_start(bmc[:], bm.rearrange("(n a) -> n a", a=1)).then_inc(consts, 16)
            sp.dma_start(erev[:], c["c_erev"]).then_inc(consts, 16)
            sp.wait_ge(zeroed, 1)
            for s in range(S):
                sp.dma_start(emb_bd[s * SD:(s + 1) * SD, s * E:(s + 1) * E], emb).then_inc(consts, 16)
            sp.wait_ge(xT_ready, 2)
            sp.dma_start(xnT_dram[0], xT[:]).then_inc(xT_stored, 16)
            with sp.Fori(0, CHUNKS - 1) as i:
                sp.wait_ge(xT_ready, i + 3)
                sp.dma_start(xnT_dram[i + 1], xT[:]).then_inc(xT_stored, 16)
                sp.wait_ge(gT_ready, i + 2)
                sp.dma_start(gT_dram[i], gT[:]).then_inc(gT_stored, 16)
            sp.wait_ge(gT_ready, CHUNKS + 1)
            sp.dma_start(gT_dram[CHUNKS - 1], gT[:]).then_inc(gT_stored, 16)
            sp.wait_ge(xT_stored, 16 * CHUNKS + 16)
            sp.wait_ge(gT_stored, 16 * CHUNKS + 16)

        @block.gpsimd
        def _(pool):
            nc.gpsimd.memset(emb_bd[:], 0.0).then_inc(zeroed, 1)
            pool.sem_inc(prob_ready, 1)

            def chunk(i):
                pool.wait_ge(gates_ready, i + 1)
                pool.wait_ge(rinv_ready, i + 1)
                nc.gpsimd.tensor_tensor(prob[:], ex[:], bc(red[:, 5, :]), ALU.mult).then_inc(prob_ready, 1)

            with pool.Fori(0, CHUNKS) as i:
                chunk(i)

        @block.vector
        def _(dve):
            done = [0]

            def link(ins, before=0):
                done[0] += 1
                ins.then_inc(step, 1)
                dve.wait_ge(step, before + done[0])

            dve.sem_inc(gates_ready, 1)
            dve.sem_inc(diff_ready, 1)
            for j in range(QUARTERS):
                dve.wait_ge(x_loaded[j], 16)
                with dve.Fori(0, KQ - 1) as k:
                    nc.vector.bn_stats(stats[:, k + j * KQ, :], x_all[:, k + j * KQ, :])
                last = nc.vector.bn_stats(stats[:, (j + 1) * KQ - 1, :], x_all[:, (j + 1) * KQ - 1, :])
            link(last)
            mean, var, dm, rstd, nmr = (small[:, j, :] for j in range(5))
            link(nc.vector.tensor_tensor(mean, stats[:, :, 1], stats[:, :, 4], ALU.add))
            link(nc.vector.tensor_tensor(dm, stats[:, :, 1], stats[:, :, 4], ALU.subtract))
            link(nc.vector.tensor_tensor(dm, dm, dm, ALU.mult))
            link(nc.vector.tensor_tensor(var, stats[:, :, 2], stats[:, :, 5], ALU.add))
            link(nc.vector.tensor_scalar(var, var, 1.0 / D, EPS, ALU.mult, ALU.add))
            nc.vector.scalar_tensor_tensor(out=var, in0=dm, scalar=0.25, in1=var, op0=ALU.mult,
                                           op1=ALU.add).then_inc(var_ready, 1)
            dve.wait_ge(std_ready, 1)
            link(nc.vector.reciprocal(rstd, rstd))
            link(nc.vector.scalar_tensor_tensor(out=nmr, in0=mean, scalar=-0.5, in1=rstd, op0=ALU.mult,
                                                op1=ALU.mult))
            LINKS = 12

            def normalise(i):
                dve.wait_ge(xT_psum, i + 1)
                for j in range(4):
                    last = nc.vector.tensor_scalar(xn[:, j, :], x_all[:, i * 4 + j, :],
                                                   small[:, 3, bass.ds(i * 4 + j, 1)],
                                                   small[:, 4, bass.ds(i * 4 + j, 1)], ALU.mult, ALU.add)
                last.then_inc(xn_ready, 1)

            rmax, ridx, rmax2, ridx2, rsum, rinv = (red[:, j, :] for j in range(6))
            erev_b = erev[:].unsqueeze(1).broadcast_to([P, G, E])
            before_gates = done[0]

            def gates(i):
                lg = pL[:].rearrange("p (g e) -> p g e", e=E)
                done[0] = before_gates
                n = LINKS * i
                dve.wait_ge(lg_psum, i + 2)
                link(nc.vector.tensor_reduce(rmax, lg, AX, ALU.max), n)
                nc.vector.tensor_tensor(logit[:], lg, bc(rmax), ALU.subtract).then_inc(diff_ready, 1)
                dve.wait_ge(diff_ready, i + 2)
                link(nc.vector.scalar_tensor_tensor(out=t1[:], in0=logit[:], scalar=0.0, in1=erev_b,
                                                    op0=ALU.is_equal, op1=ALU.mult), n)
                link(nc.vector.tensor_reduce(ridx, t1[:], AX, ALU.max), n)
                link(nc.vector.tensor_tensor(first[:], t1[:], bc(ridx), ALU.is_equal), n)
                dve.wait_ge(ex_ready, i + 1)
                link(nc.vector.tensor_reduce(rsum, ex[:], AX, ALU.add), n)
                nc.vector.reciprocal(rinv, rsum).then_inc(rinv_ready, 1)
                link(nc.vector.scalar_tensor_tensor(out=logit[:], in0=first[:], scalar=MASKED, in1=logit[:],
                                                    op0=ALU.mult, op1=ALU.add), n)
                link(nc.vector.tensor_reduce(rmax2, logit[:], AX, ALU.max), n)
                link(nc.vector.tensor_tensor(t1[:], logit[:], bc(rmax2), ALU.is_equal), n)
                link(nc.vector.tensor_tensor(t1[:], t1[:], erev_b, ALU.mult), n)
                link(nc.vector.tensor_reduce(ridx2, t1[:], AX, ALU.max), n)
                link(nc.vector.tensor_tensor(t1[:], t1[:], bc(ridx2), ALU.is_equal), n)
                link(nc.vector.tensor_tensor(first[:], first[:], t1[:], ALU.add), n)
                dve.wait_ge(gT_psum, i + 1)
                dve.wait_ge(prob_ready, i + 2)
                nc.vector.tensor_tensor(gate[:], prob[:], first[:], ALU.mult).then_inc(gates_ready, 1)
                assert done[0] == before_gates + LINKS

            normalise(0)
            with dve.Fori(0, CHUNKS - 1) as i:
                normalise(i + 1)
                gates(i)
            gates(CHUNKS - 1)

        @block.scalar
        def _(act):
            act.sem_inc(xT_ready, 1)
            act.sem_inc(hT_ready, 1)
            act.sem_inc(gT_ready, 1)
            act.wait_ge(var_ready, 1)
            nc.scalar.activation(small[:, 3, :], small[:, 1, :], ACT.Sqrt).then_inc(std_ready, 1)
            act.wait_ge(consts, 16 * N_CONST)

            def transpose_read(i):
                act.wait_ge(xT_stored, i * 16 + 16)
                act.wait_ge(xT_psum, i + 2)
                nc.scalar.activation(xT[:], pT[:], ACT.Copy).then_inc(xT_ready, 1)
                act.wait_ge(lg_psum, i + 1)
                act.wait_ge(hT_psum, i + 1)
                nc.scalar.activation(hT[:], pH[:], ACT.Identity, bias=bmc[:]).then_inc(hT_ready, 1)

            def gates(i):
                act.wait_ge(prob_ready, i + 1)
                act.wait_ge(diff_ready, i + 2)
                nc.scalar.activation(ex[:], logit[:], ACT.Exp).then_inc(ex_ready, 1)
                act.wait_ge(gT_stored, i * 16 + 16)
                act.wait_ge(gT_psum, i + 2)
                nc.scalar.activation(gT[:], pG[:], ACT.Copy).then_inc(gT_ready, 1)

            transpose_read(0)
            with act.Fori(0, CHUNKS - 1) as i:
                transpose_read(i + 1)
                gates(i)
            gates(CHUNKS - 1)

        @block.tensor
        def _(pe):
            pe.sem_inc(xT_psum, 1)
            pe.sem_inc(lg_psum, 1)
            pe.sem_inc(gT_psum, 1)
            pe.wait_ge(consts, 16 * N_CONST)

            def logits(i):
                pe.wait_ge(xT_ready, i + 1)
                pe.wait_ge(xn_ready, i + 1)
                for j in range(4):
                    last = nc.tensor.transpose(pT[:, j * P:(j + 1) * P], xn[:, j, :], ident[:])
                last.then_inc(xT_psum, 1)
                pe.wait_ge(hT_ready, i + 1)
                pe.wait_ge(xT_ready, i + 2)
                nc.tensor.matmul(pH[:], wm[:], xT[:], start=True, stop=True).then_inc(hT_psum, 1)
                pe.wait_ge(diff_ready, i + 1)
                pe.wait_ge(hT_ready, i + 2)
                for j in range(4):
                    last = nc.tensor.matmul(pL[:, j * P:(j + 1) * P], hT[:, j * P:(j + 1) * P], emb_bd[:],
                                            start=True, stop=True)
                last.then_inc(lg_psum, 1)

            def gates(i):
                pe.wait_ge(gT_ready, i + 1)
                pe.wait_ge(gates_ready, i + 2)
                for j in range(4):
                    last = nc.tensor.transpose(pG[:, j * P:(j + 1) * P],
                                               gate[:, j * S:(j + 1) * S, :].rearrange("p g e -> p (g e)"), ident[:])
                last.then_inc(gT_psum, 1)

            logits(0)
            with pe.Fori(0, CHUNKS - 1) as i:
                logits(i + 1)
                gates(i)
            gates(CHUNKS - 1)


def experts(nc, x, Wm, bm, W1, b1, W2, b2, Wo, bo, c, xnT_dram, gT_dram, xf_dram):
    with ExitStack() as ctx:
        def sb(name, shape, dt=F32):
            return ctx.enter_context(nc.sbuf_tensor(name, shape, dt))

        def ps(name, shape):
            return ctx.enter_context(nc.psum_tensor(name, shape, F32))

        def sem(name):
            return ctx.enter_context(nc.semaphore(name))

        PARTS = 4
        SP = S // 2
        Q = 2 * SD
        UNITS = 2 * S
        EU = EP // 2
        HB, AB = 3, 8
        BEHIND = 3

        ident = sb("e_ident", [P, P])
        wm_rep = sb("wm_rep", [D, SP, PARTS, Q])
        bm_rep = sb("bm_rep", [P, SP])
        w1f = sb("w1f", [P, 2, E * I])
        w1r = sb("w1r", [P, 2, EP, 2 * I], F32R)
        b1c = sb("b1c", [P, EP])
        w2p = sb("w2p", [P, EP, 2 * SD])
        b2c = sb("b2c", [P, 2])
        wo_rep = sb("wo_rep", [P, S, D])
        boc = sb("boc", [P, 1])
        self_ = sb("self", [P, UNITS, P])
        selr = sb("selr", [P, UNITS, P], F32R)
        xT = sb("e_xT", [P, CH])
        gT = sb("e_gT", [P, CH])
        xr = sb("e_xr", [P, CH // P, D])
        tt = sb("tt", [P, CH])
        tr = sb("tr", [P, 2, SP, CH], F32R)
        g_hi = sb("g_hi", [P, 2, CH], F32R)
        g_lo = sb("g_lo", [P, 2, CH], F32R)
        hid = sb("e_hid", [P, AB, CH])
        gs = sb("gs", [P, 2, CH])
        z = sb("z", [P, 2, CH])
        yT = sb("yT", [P, CH])
        xf = sb("xf", [P, CH // P, D])

        p_hid = ps("e_phid", [P, HB, CH])
        p_eo = ps("p_eo", [P, 2, CH])
        p_g = ps("p_g", [P, CH])
        p_y = ps("p_y", [P, CH])
        p_m = ps("p_m", [P, CH])

        zeroed = sem("e_zeroed")
        consts = sem("e_consts")
        slot_consts = sem("slot_consts")
        w1_loaded = sem("w1_loaded")
        sel_loaded = sem("sel_loaded")
        w1_hi = sem("w1_hi")
        weights = sem("weights")
        xT_loaded = sem("e_xT_loaded")
        gT_loaded = sem("gT_loaded")
        xr_loaded = sem("e_xr_loaded")
        t_psum = sem("t_psum")
        t_ready = sem("t_ready")
        tr_hi = sem("tr_hi")
        tr_ready = sem("tr_ready")
        g_hi_ready = sem("g_hi_ready")
        g_split = sem("g_split")
        up_done = sem("up_done")
        gelu_done = sem("e_gelu_done")
        down_done = sem("down_done")
        g_psum = sem("g_psum")
        g_ready = sem("g_ready")
        z_ready = sem("z_ready")
        wo_done = sem("wo_done")
        yT_ready = sem("yT_ready")
        y_psum = sem("y_psum")
        xf_ready = sem("xf_ready")
        xf_stored = sem("xf_stored")

        N_SLOT = 2 * PARTS
        N_W1 = 2 * PARTS
        N_CONST = 1 + 2 + 2 + 1 + E // 2 + 1

        def over_chunks(eng, chunk):
            with eng.Fori(0, CHUNKS // 2 - 1) as i:
                chunk(2 * i, 0, False)
                chunk(2 * i + 1, 1, False)
            chunk(CHUNKS - 2, 0, False)
            chunk(CHUNKS - 1, 1, True)

        block = ctx.enter_context(nc.Block())

        @block.sync
        def _(sp):
            sp.sem_inc(xf_stored, 16)
            sp.dma_start(xT[:], xnT_dram[0]).then_inc(xT_loaded, 16)
            for part in range(PARTS):
                sp.dma_start(wm_rep[:, :, part, :], Wm.rearrange("k (s q) -> k s q", q=Q)).then_inc(slot_consts, 16)
                sp.dma_start(bm_rep[part * Q:(part + 1) * Q, :], bm.rearrange("(s q) -> q s", q=Q),
                             allow_slow_non_contiguous=True).then_inc(slot_consts, 16)
            sp.wait_ge(zeroed, 1)
            for part in range(PARTS):
                for s in range(2):
                    r = part * Q + s * SD
                    sp.dma_start(w1f[r:r + SD, s, :].rearrange("d (e i) -> d e i", i=I),
                                 W1.rearrange("e d i -> d e i")).then_inc(w1_loaded, 16)
            sp.dma_start(self_[:], c["c_sel"].rearrange("p (u k) -> p u k", k=P)).then_inc(sel_loaded, 16)
            sp.dma_start(gT[:], gT_dram[0]).then_inc(gT_loaded, 16)
            sp.dma_start(ident[:], c["c_ident"]).then_inc(consts, 16)
            sp.wait_ge(zeroed, 2)
            w2v = W2.rearrange("(ep two) i o -> two i ep o", two=2)
            b1v = b1.rearrange("(ep two) i -> two i ep", two=2)
            for e in range(2):
                sp.dma_start(w2p[e * I:(e + 1) * I, :, e * SD:(e + 1) * SD], w2v[e]).then_inc(consts, 16)
                sp.dma_start(b1c[e * I:(e + 1) * I, :], b1v[e], allow_slow_non_contiguous=True).then_inc(consts, 16)
            sp.dma_start(b2c[:], b2.rearrange("(h e) o -> (e o) h", h=2), allow_slow_non_contiguous=True)\
                .then_inc(consts, 16)
            for e in range(E // 2):
                sp.dma_start(wo_rep[e * SD:(e + 1) * SD, :, :], Wo.rearrange("(s o) n -> o s n", o=SD))\
                    .then_inc(consts, 16)
            sp.dma_start(boc[:], bo.rearrange("(n a) -> n a", a=1)).then_inc(consts, 16)

            def chunk(n, par, last):
                if not last:
                    sp.wait_ge(t_psum, 4 * n + 4)
                    sp.dma_start(xT[:], xnT_dram[n + 1]).then_inc(xT_loaded, 16)
                    sp.wait_ge(g_split, n + 1)
                    sp.dma_start(gT[:], gT_dram[n + 1]).then_inc(gT_loaded, 16)
                sp.wait_ge(xf_ready, n + 1)
                sp.dma_start(xr[:], x.rearrange("(c k p) n -> c p k n", k=CH // P, p=P)[n]).then_inc(xr_loaded, 16)
                sp.wait_ge(xf_ready, n + 2)
                sp.dma_start(xf_dram.rearrange("(c k p) n -> c p k n", k=CH // P, p=P)[n], xf[:])\
                    .then_inc(xf_stored, 16)

            over_chunks(sp, chunk)
            sp.wait_ge(xf_stored, 16 * CHUNKS + 16)

        @block.gpsimd
        def _(pool):
            nc.gpsimd.memset(w1f[:], 0.0).then_inc(zeroed, 1)
            nc.gpsimd.memset(w2p[:], 0.0).then_inc(zeroed, 1)
            pool.wait_ge(sel_loaded, 16)
            nc.gpsimd.tensor_copy(selr[:], self_[:]).then_inc(weights, 1)

        @block.scalar
        def _(act):
            act.sem_inc(gelu_done, HB)
            act.wait_ge(slot_consts, 16 * N_SLOT)

            def slots(n, k):
                act.wait_ge(tr_ready, 4 * n + k + 1)
                act.wait_ge(t_psum, 4 * n + k + 1)
                nc.scalar.activation(tt[:], p_m[:], ACT.Identity, bias=bm_rep[:, k:k + 1]).then_inc(t_ready, 1)

            for k in range(SP):
                slots(0, k)
            act.wait_ge(consts, 16 * N_CONST)

            def chunk(n, par, last):
                for u in range(UNITS):
                    for q in range(EU):
                        j = EU * u + q
                        k = 64 * n + j
                        act.wait_ge(up_done, k + 1)
                        act.wait_ge(down_done, k + 1)
                        ep = (u % 2) * EU + q
                        nc.scalar.activation(hid[:, j % AB, :], p_hid[:, j % HB, :], ACT.Gelu,
                                             bias=b1c[:, ep:ep + 1]).then_inc(gelu_done, 1)
                    if not last and u % 2 == 0 and 2 <= u <= 8:
                        slots(n + 1, u // 2 - 1)

            over_chunks(act, chunk)

        @block.vector
        def _(dve):
            dve.sem_inc(tr_ready, 1)
            dve.sem_inc(g_ready, 1)
            dve.sem_inc(z_ready, 2)
            dve.sem_inc(yT_ready, 1)
            dve.sem_inc(xf_ready, 1)
            dve.wait_ge(w1_loaded, 16 * N_W1)
            nc.vector.tensor_copy(w1r[:].rearrange("p s e i -> p s (e i)"), w1f[:]).then_inc(w1_hi, 1)
            dve.wait_ge(w1_hi, 1)
            for part in (1, 3):
                r = slice(part * Q, (part + 1) * Q)
                w = w1r[r].rearrange("p s e i -> p s (e i)")
                nc.vector.tensor_tensor(w, w1f[r], w.bitcast(F32), ALU.subtract).then_inc(weights, 1)

            def split_slots(n, par, k):
                if not isinstance(n, int) or n:
                    dve.wait_ge(up_done, 64 * n - 63)
                dve.wait_ge(t_ready, 4 * n + k + 1)
                nc.vector.tensor_copy(tr[:, par, k, :], tt[:]).then_inc(tr_hi, 1)
                dve.wait_ge(tr_hi, 4 * n + k + 1)
                low = tr[P // 2:, par, k, :]
                nc.vector.tensor_tensor(low, tt[P // 2:, :], low.bitcast(F32), ALU.subtract).then_inc(tr_ready, 1)

            def split_gates(n, par):
                if not isinstance(n, int) or n:
                    dve.wait_ge(g_psum, 16 * n - 15)
                dve.wait_ge(gT_loaded, 16 * n + 16)
                nc.vector.tensor_copy(g_hi[:, par, :], gT[:]).then_inc(g_hi_ready, 1)
                dve.wait_ge(g_hi_ready, n + 1)
                nc.vector.tensor_tensor(g_lo[:, par, :], gT[:], g_hi[:, par, :].bitcast(F32), ALU.subtract)\
                    .then_inc(g_split, 1)

            for k in range(SP):
                split_slots(0, 0, k)
            split_gates(0, 0)
            dve.wait_ge(consts, 16 * N_CONST)

            def chunk(n, par, last):
                for u in range(UNITS):
                    g = 16 * n + u
                    dve.wait_ge(g_psum, g + 1)
                    nc.vector.tensor_copy(gs[:, u % 2, :], p_g[:]).then_inc(g_ready, 1)
                    dve.wait_ge(wo_done, g + 1)
                    dve.wait_ge(down_done, 4 * g + 4 + AB)
                    dve.wait_ge(g_ready, g + 1 + 1)
                    nc.vector.scalar_tensor_tensor(out=z[:, u % 2, :], in0=p_eo[:, u % 2, :],
                                                   scalar=b2c[:, u % 2:u % 2 + 1], in1=gs[:, u % 2, :],
                                                   op0=ALU.add, op1=ALU.mult).then_inc(z_ready, 1)
                    if not last and u % 2 == 0 and 2 <= u <= 8:
                        split_slots(n + 1, 1 - par, u // 2 - 1)
                    if not last and u == 10:
                        split_gates(n + 1, 1 - par)
                dve.wait_ge(wo_done, 16 * n + 16 + 2)
                dve.wait_ge(y_psum, n + 1)
                nc.vector.tensor_scalar(yT[:], p_y[:], boc[:], None, ALU.add).then_inc(yT_ready, 1)
                dve.wait_ge(xf_stored, 16 * n + 16)
                dve.wait_ge(xr_loaded, 16 * n + 16)
                dve.wait_ge(y_psum, n + 2)
                nc.vector.tensor_tensor(xf[:], p_m[:].rearrange("p (k n) -> p k n", n=D), xr[:], ALU.add)\
                    .then_inc(xf_ready, 1)

            over_chunks(dve, chunk)

        @block.tensor
        def _(pe):
            pe.sem_inc(down_done, AB)
            pe.sem_inc(wo_done, 2)
            pe.sem_inc(y_psum, 1)
            pe.wait_ge(slot_consts, 16 * N_SLOT)

            def slots(n, k):
                if k:
                    pe.wait_ge(t_ready, 4 * n + k)
                elif not isinstance(n, int) or n:
                    pe.wait_ge(xf_ready, n)
                pe.wait_ge(xT_loaded, 16 * n + 16)
                nc.tensor.matmul(p_m[:], wm_rep[:, k].rearrange("p a q -> p (a q)"), xT[:],
                                 start=True, stop=True).then_inc(t_psum, 1)

            for k in range(SP):
                slots(0, k)
            pe.wait_ge(consts, 16 * N_CONST)
            pe.wait_ge(weights, 3)

            def chunk(n, par, last):
                pe.wait_ge(g_split, n + 1)
                pe.wait_ge(tr_ready, 4 * n + 4 + 1)

                def down(j):
                    u, q = divmod(j, EU)
                    if q == 0:
                        pe.wait_ge(z_ready, 16 * n + u + 1)
                    pe.wait_ge(gelu_done, 64 * n + j + 1 + HB)
                    nc.tensor.matmul(p_eo[q * 2 * SD:(q + 1) * 2 * SD, u % 2, :], w2p[:, (u % 2) * EU + q, :],
                                     hid[:, j % AB, :], start=True, stop=True).then_inc(down_done, 1)

                def project(u):
                    if u == 0:
                        pe.wait_ge(yT_ready, n + 1)
                    pe.wait_ge(z_ready, 16 * n + u + 1 + 2)
                    nc.tensor.matmul(p_y[:], wo_rep[:, u // 2, :], z[:, u % 2, :],
                                     start=(u == 0), stop=(u == UNITS - 1)).then_inc(wo_done, 1)

                for u in range(UNITS):
                    s = u // 2
                    for q in range(EU):
                        j = EU * u + q
                        pe.wait_ge(gelu_done, 64 * n + (j + 1 if j >= HB else HB))
                        nc.tensor.matmul(p_hid[:, j % HB, :], w1r[:, s % 2, (u % 2) * EU + q, :],
                                         tr[:, par, s // 2, :], start=True, stop=True).then_inc(up_done, 1)
                        if j >= BEHIND:
                            down(j - BEHIND)
                        if q == 0 and u >= 2:
                            project(u - 2)
                        if q == 2:
                            pe.wait_ge(g_ready, 16 * n + u + 1)
                            nc.tensor.matmul(p_g[:], selr[:, u, :], g_hi[:, par, :], start=True, stop=False)
                            nc.tensor.matmul(p_g[:], selr[:, u, :], g_lo[:, par, :], start=False, stop=True)\
                                .then_inc(g_psum, 1)
                    if not last and u % 2 == 0 and 2 <= u <= 8:
                        slots(n + 1, u // 2 - 1)
                for j in range(EU * UNITS - BEHIND, EU * UNITS):
                    down(j)
                project(UNITS - 2)
                project(UNITS - 1)
                if not last:
                    pe.wait_ge(t_ready, 4 * n + 8)
                pe.wait_ge(yT_ready, n + 2)
                for k in range(CH // P):
                    last_t = nc.tensor.transpose(p_m[:, k * P:(k + 1) * P], yT[:, k * P:(k + 1) * P], ident[:])
                last_t.then_inc(y_psum, 1)

            over_chunks(pe, chunk)


def attention(nc, w_qkv, w_o, log_p, log_a, w1, b1, w2, b2, c, xnT_dram, xf_dram, out):
    with ExitStack() as ctx:
        def sb(name, shape, dt=F32):
            return ctx.enter_context(nc.sbuf_tensor(name, shape, dt))

        def ps(name, shape):
            return ctx.enter_context(nc.psum_tensor(name, shape, F32))

        def sem(name):
            return ctx.enter_context(nc.semaphore(name))

        HC = HALF * C
        HH = HALF * H

        ident = sb("a_ident", [P, P])
        wqkv = sb("wqkv", [D, 3 * H * HD])
        wo = sb("wo", [P, PAIRS, D])
        w_up = sb("w_up", [P, 2, HC])
        w_down = sb("w_down", [HC, HH])
        cols = sb("cols", [P, 12])
        cos = sb("cos", [P, L])
        sin = sb("sin", [P, L])
        ker_mask = sb("ker_mask", [P, L])
        xa = sb("xa", [P, 2, RING, L])
        std = sb("std", [P, H, L + (QB - 1) * P])
        hid = sb("hid", [P, HIDS, 2, L])
        pr = sb("pr", [P, TILES, L])
        pT = sb("pT", [P, QB, H, GQ])
        vv = sb("vv", [P, QB, H * HD])
        kk = sb("kk", [P, PAIRS, L])
        raw = sb("raw", [P, 2, PAIRS, P])
        rot = sb("rot", [P, 2, PAIRS, P])
        xT = sb("a_xT", [P, QB, P])
        oT = sb("oT", [P, PAIRS, P])
        xf = sb("a_xf", [P, D])
        y = sb("y", [P, D])
        mx = sb("mx", [P, TILES])
        nmx = sb("nmx", [P, TILES])
        sums = sb("sums", [P, TILES])
        rsum = sb("rsum", [P, TILES])
        room = pT[:].rearrange("p k h n -> p (k h n)")
        dist, mask, ker = (room[:, k * L:(k + 1) * L] for k in range(3))

        p_up = ps("p_up", [P, 2, 2, L])
        p_down = ps("p_down", [P, 2, L])
        p_gap = ps("p_gap", [P, 2, L])

        zeroed = sem("a_zeroed")
        wqkv_loaded = sem("wqkv_loaded")
        angles = sem("angles")
        ker_consts = sem("ker_consts")
        consts = sem("a_consts")
        pr_zeroed = sem("pr_zeroed")
        sp_abs = sem("sp_abs")
        sp_exp = sem("sp_exp")
        sp_ln = sem("sp_ln")
        sp_sum = sem("sp_sum")
        ker_ln = sem("ker_ln")
        ker_ready = sem("ker_ready")
        tables = sem("tables")
        ker_placed = sem("ker_placed")
        xT_loaded = [sem(f"xT_loaded{i}") for i in range(QB)]
        xf_loaded = sem("a_xf_loaded")
        rot_loaded = sem("rot_loaded")
        ropeq = sem("ropeq")
        ropek = sem("ropek")
        qstep = sem("qstep")
        kstep = sem("kstep")
        x_loaded = [sem(f"a_x_loaded{i}") for i in range(RING)]
        up_done = sem("a_up_done")
        gelu_done = sem("a_gelu_done")
        down_done = sem("a_down_done")
        sc_ready = sem("sc_ready")
        logit_turn = sem("logit_turn")
        norm_turn = sem("norm_turn")
        load_turn = sem("load_turn")
        pool_turn = sem("pool_turn")
        logit_done = sem("logit_done")
        nmx_ready = sem("nmx_ready")
        exp_done = sem("exp_done")
        rsum_ready = sem("rsum_ready")
        norm_done = sem("norm_done")
        gap_fill = sem("gap_fill")
        gap_read = sem("gap_read")
        y_stored = sem("y_stored")

        N_KER = 5
        N_CONST = 3 + 2 * 2 * HALF + HALF
        PROLOGUE = 4 + H + 4

        def fillers(ib, r, more):
            first = sum(SCORES_BESIDE[:r])
            n = 2 * (ib + 1)
            return ([("scores", h) for h in range(first, first + SCORES_BESIDE[r]) if more] +
                    [("t0", u) for u in range(n) if 3 + u * (GT - 3) // n == r])

        def fillers_before(ib, r):
            n = 2 * ((ib - 1) % QB + 1)
            return [u for u in range(n) if 2 + u * 4 // n == r]

        def plan(last_batch):
            at, base = {}, PROLOGUE - (2 * QB + 2)
            for ib in range(QB + 1):
                more = not (last_batch and ib == QB - 1)
                more2 = not (last_batch and ib >= QB - 2)
                ends = [("t1", u) for u in range(2 * ((ib - 1) % QB + 1))] + [("pv1", 0)]
                if ib == QB:
                    units = ends + [("o", 0)]
                else:
                    units = ends + [("v", 0), ("o", 0), ("v", 1)]
                    for r in range(GT):
                        units += fillers(ib, r, more)
                    units += [("pv0", 0)] + [("qk", j) for j in range(4 if more2 else 0)]
                for k, u in enumerate(units):
                    at[ib, u] = base + k
                base += len(units)
                if ib == QB - 1:
                    per_batch = base - (PROLOGUE - (2 * QB + 2))
            return at, per_batch

        UNITS, PER_BATCH = plan(False)
        UNITS_LAST, _ = plan(True)

        def unit(b, ib, kind, k=0):
            at = (UNITS_LAST if isinstance(b, int) and b == B - 1 else UNITS)[ib, (kind, k)]
            if is_first(b, ib) and (kind, k) == ("v", 0):
                at += 1
            return PER_BATCH * b + at, at % 2

        assert PER_BATCH % 2 == 0

        def over_batches(eng, step):
            step(0, 0, False)
            with eng.Fori(0, B - 1) as b:
                for ib in range(1, QB):
                    step(b, ib, False)
                step(b + 1, 0, False)
            for ib in range(1, QB):
                step(B - 1, ib, True)

        def before(b, ib):
            return (b, ib - 1) if ib else (b - 1, QB - 1)

        def is_first(b, ib):
            return isinstance(b, int) and b == 0 and ib == 0

        def ahead(b, ib, m):
            return (b, ib + m) if ib + m < QB else (b + 1, ib + m - QB)

        def window(t):
            return slice(L - TQ * (t + 1), L)

        def keys(ib, t):
            return slice(L - (ib + 1) * P, L - P + TQ * (t + 1))

        def std_keys(ib, n_keys):
            first = 0 if ib % 2 else L
            return slice(first, first + n_keys)

        def by_query(a):
            return a.rearrange("p (t i) -> p i t", i=TQ)

        def wide(table):
            return table.unsqueeze(1).broadcast_to([P, PAIRS, P])

        block = ctx.enter_context(nc.Block())

        @block.sync
        def _(sp):
            sp.dma_start(wqkv[:], w_qkv).then_inc(wqkv_loaded, 16)
            sp.dma_start(xT[:, 0, :], xnT_dram[0, :, 0:P]).then_inc(xT_loaded[0], 16)
            sp.dma_start(xT[:, 1, :], xnT_dram[0, :, P:2 * P]).then_inc(xT_loaded[1], 16)
            sp.dma_start(cos[:], c["c_cos"]).then_inc(angles, 16)
            sp.dma_start(sin[:], c["c_sin"]).then_inc(angles, 16)
            sp.dma_start(dist, c["c_dist"]).then_inc(ker_consts, 16)
            sp.dma_start(mask, c["c_mask"]).then_inc(ker_consts, 16)
            by_head = lambda v: v.unsqueeze(0).broadcast_to([TQ, H, 1])
            sp.dma_start(cols[:, 0:1], by_head(log_p)).then_inc(ker_consts, 16)
            sp.dma_start(cols[:, 1:2], by_head(log_a)).then_inc(ker_consts, 16)
            sp.dma_start(cols[:, 2:3], by_head(b2.rearrange("(n a) -> n a", a=1))).then_inc(ker_consts, 16)
            sp.dma_start(cols[:, 3:4], b1.rearrange("(n a) -> n a", a=1).unsqueeze(0).broadcast_to([HALF, C, 1]))\
                .then_inc(consts, 16)
            sp.dma_start(ident[:], c["c_ident"]).then_inc(consts, 16)
            def rotate():
                for h in range(4):
                    to, fr = h * 32, (h ^ 1) * 32
                    sp.dma_start(rot[to:to + 32], raw[fr:fr + 32]).then_inc(rot_loaded, 16)

            sp.wait_ge(gap_read, 4 + 2)
            rotate()
            sp.wait_ge(zeroed, 1)
            for i in range(HALF):
                sp.dma_start(w_down[i * C:(i + 1) * C, i * H:(i + 1) * H], w2).then_inc(consts, 16)
                for half in range(2):
                    for kind in range(2):
                        r = HH * (half ^ kind) + i * H
                        sp.dma_start(w_up[r:r + H, half, i * C:(i + 1) * C], w1[kind * H:(kind + 1) * H, :])\
                            .then_inc(consts, 16)
            sp.dma_start(wo[:], w_o.rearrange("(c k) n -> k c n", k=P)).then_inc(consts, 16)
            sp.wait_ge(ker_ready, 1)
            for r in range(RING):
                sp.dma_start(xa[HH:, 0, r, :], ker[:HH, :]).then_inc(ker_placed, 16)
                sp.dma_start(xa[:HH, 1, r, :], ker[HH:, :]).then_inc(ker_placed, 16)
            sp.wait_ge(ker_placed, 16 * 2 * RING)

            def load(b, ib, t):
                g = 64 * b + (16 * ib + t)
                n_keys = TQ * (16 * ib + t + 1)
                sp.wait_ge(up_done, g + 1)
                sp.wait_ge(sc_ready, g + 1)
                for half in range(2):
                    fr = P // 2 * half + t
                    sp.dma_start(xa[HH * half:HH * half + HH, half, t % RING, window(16 * ib + t)],
                                 std[fr:fr + 3 * TILES + 1:TILES, :, std_keys(ib, n_keys)])\
                        .then_inc(x_loaded[t % RING], 16)

            sp.sem_inc(y_stored, 16)
            sp.wait_ge(gap_read, 4 + H + 2)
            for t in range(RING):
                load(0, 0, t)
            sp.wait_ge(gap_read, PROLOGUE + 2)

            out_rows = out.rearrange("(b k p) n -> b k p n", k=QB, p=P)
            xf_rows = xf_dram.rearrange("(b k p) n -> b k p n", k=QB, p=P)

            def store(b, ib):
                if is_first(b, ib):
                    return
                sp.wait_ge(gap_read, unit(b, ib, "o")[0] + 1 + 2)
                sp.sem_inc(load_turn, 1)
                rows = out_rows[b, ib - 1] if ib else out_rows[b - 1, QB - 1]
                sp.dma_start(rows, y[:]).then_inc(y_stored, 16)

            def step(b, ib, last):
                more = not (last and ib == QB - 1)
                for t in range(RING, TILES):
                    load(b, ib, t)
                    if t == 5 and more:
                        if not is_first(b, ib):
                            sp.wait_ge(gap_read, unit(*before(b, ib), "qk", 3)[0] + 1 + 2)
                            sp.sem_inc(load_turn, 1)
                        rotate()
                    if t == 8 and not (last and ib >= QB - 2):
                        bn, ibn = ahead(b, ib, 2)
                        sp.dma_start(xT[:, ibn, :], xnT_dram[bn, :, ibn * P:(ibn + 1) * P]).then_inc(xT_loaded[ibn], 16)
                    if t == GT + RING - 1:
                        store(b, ib)
                        sp.dma_start(xf[:], xf_rows[b, ib]).then_inc(xf_loaded, 16)
                if more:
                    sp.wait_ge(gap_read, unit(b, ib, "pv0")[0] + 2)
                    sp.sem_inc(load_turn, 1)
                    for t in range(RING):
                        load(*ahead(b, ib, 1), t)
            over_batches(sp, step)
            store(B - 1, QB)
            sp.wait_ge(y_stored, 16 * BLOCKS + 16)

        @block.gpsimd
        def _(pool):
            nc.gpsimd.memset(w_up[:], 0.0)
            nc.gpsimd.memset(w_down[:], 0.0).then_inc(zeroed, 1)
            nc.gpsimd.memset(pr[:], 0.0).then_inc(pr_zeroed, 1)
            pool.sem_inc(sc_ready, RING)
            pool.wait_ge(pr_zeroed, 1)
            pool.wait_ge(angles, 32)

            def rope_keys(b, ib):
                m = 4 * b + ib
                cs = slice(ib * P, (ib + 1) * P)
                pool.wait_ge(rot_loaded, 64 * m + 64)
                nc.gpsimd.tensor_tensor(raw[:, 1], raw[:, 1], wide(cos[:, cs]), ALU.mult).then_inc(kstep, 1)
                nc.gpsimd.tensor_tensor(rot[:, 1], rot[:, 1], wide(sin[:, cs]), ALU.mult).then_inc(kstep, 1)
                pool.wait_ge(kstep, 2 * m + 2)
                nc.gpsimd.tensor_tensor(kk[:, :, cs], raw[:, 1], rot[:, 1], ALU.add).then_inc(ropek, 1)

            rope_keys(0, 0)
            pool.wait_ge(ropek, 1)
            pool.wait_ge(tables, 1)

            def step(b, ib, last):
                more = not (last and ib == QB - 1)
                for t in range(TILES):
                    w, wx = keys(ib, t), window(16 * ib + t)
                    if t % GT == 0 and not is_first(b, ib):
                        if t:
                            pool.wait_ge(gap_read, unit(b, ib, "pv1")[0] + 2)
                        else:
                            pool.wait_ge(gap_read, unit(*before(b, ib), "pv0")[0] + 2)
                        pool.sem_inc(pool_turn, 1)
                    pool.wait_ge(x_loaded[t % RING], 32 * (64 // RING * b + (16 * ib + t) // RING) + 32)
                    for half in range(2):
                        r = slice(HH * half, HH * half + HH)
                        last_add = nc.gpsimd.tensor_tensor(pr[r, t, w], xa[r, half, t % RING, wx], ker_mask[r, wx],
                                                           ALU.add)
                    last_add.then_inc(sc_ready, 1)
                    if t == GT - 1 and more:
                        pool.wait_ge(sc_ready, 64 * b + (16 * ib + t + 1) + RING)
                        pool.sem_inc(pool_turn, 1)
                        rope_keys(*ahead(b, ib, 1))
                        pool.wait_ge(ropek, 4 * b + (ib + 2))
                        pool.sem_inc(pool_turn, 1)

            over_batches(pool, step)

        @block.scalar
        def _(act):
            act.sem_inc(gelu_done, 2)
            act.wait_ge(ker_consts, 16 * N_KER)
            act.wait_ge(sp_abs, 1)
            nc.scalar.activation(cols[:, 6:8], cols[:, 4:6], ACT.Exp, scale=-1.0).then_inc(sp_exp, 1)
            act.wait_ge(sp_exp, 1)
            nc.scalar.activation(cols[:, 8:10], cols[:, 6:8], ACT.Ln, bias=1.0).then_inc(sp_ln, 1)
            act.wait_ge(sp_sum, 1)
            nc.scalar.activation(ker, dist, ACT.Ln, bias=1.0, scale=cols[:, 11:12]).then_inc(ker_ln, 1)
            act.wait_ge(consts, 16 * N_CONST)

            def step(b, ib, last):
                for G in range(GROUPS):
                    for t in range(GT * G, GT * G + GT):
                        g = 64 * b + (16 * ib + t)
                        n_keys = TQ * (16 * ib + t + 1)
                        act.wait_ge(down_done, 64 * b + (16 * ib + (t + 1 if t >= HIDS else HIDS)))
                        act.wait_ge(up_done, g + 1 + RING)
                        nc.scalar.activation(hid[:, t % HIDS, :, 0:n_keys], p_up[:, t % 2, :, 0:n_keys], ACT.Gelu,
                                             bias=cols[:, 3:4]).then_inc(gelu_done, 1)
                    act.wait_ge(nmx_ready, 8 * b + (2 * ib + G) + 1)
                    for t in range(GT * G, GT * G + GT):
                        nc.scalar.activation(pr[:, t, keys(ib, t)], pr[:, t, keys(ib, t)], ACT.Exp,
                                             bias=nmx[:, t:t + 1], accum_out=sums[:, t:t + 1]).then_inc(exp_done, 1)

            over_batches(act, step)

        @block.vector
        def _(dve):
            dve.sem_inc(logit_done, 2)
            dve.sem_inc(gap_read, 2)
            def score_read(at, h, ib):
                k, bank = at(h)
                n_keys = (ib + 1) * P
                dve.wait_ge(gap_fill, k + 1)
                nc.vector.tensor_scalar(std[:, h, std_keys(ib, n_keys)], p_gap[:, bank, 0:n_keys], HD ** -0.5, None,
                                        ALU.mult).then_inc(gap_read, 1)

            def qk_read(at, m):
                for j in range(4):
                    k, bank = at(j)
                    if j == 2 and (not isinstance(m, int) or m):
                        dve.wait_ge(ropek, m)
                    dve.wait_ge(gap_fill, k + 1)
                    nc.vector.tensor_copy(raw[:, j // 2, (j % 2) * 4:(j % 2) * 4 + 4, :],
                                          p_gap[:, bank, :].rearrange("p (c n) -> p c n", n=P)).then_inc(gap_read, 1)

            def rope_queries(b, ib, part):
                m = 4 * b + ib
                cs = slice(ib * P, (ib + 1) * P)
                if part < 2:
                    if part == 0:
                        dve.wait_ge(rot_loaded, 64 * m + 64)
                    v, table = ((raw, cos), (rot, sin))[part]
                    qs = v[:, 0].rearrange("p c (i t) -> p c i t", i=TQ)
                    qt = by_query(table[:, cs]).unsqueeze(1).broadcast_to([P, PAIRS, TQ, TILES])
                    nc.vector.tensor_tensor(qs, qs, qt, ALU.mult).then_inc(qstep, 1)
                else:
                    dve.wait_ge(qstep, 2 * m + 2)
                    nc.vector.tensor_tensor(raw[:, 0], raw[:, 0], rot[:, 0], ALU.add).then_inc(ropeq, 1)

            qk_read(lambda j: (j, j % 2), 0)
            dve.wait_ge(ker_consts, 16 * N_KER)
            nc.vector.scalar_tensor_tensor(out=cols[:, 4:6], in0=cols[:, 0:2], scalar=-1.0, in1=cols[:, 0:2],
                                           op0=ALU.mult, op1=ALU.max).then_inc(sp_abs, 1)
            dve.wait_ge(sp_ln, 1)
            nc.vector.scalar_tensor_tensor(out=cols[:, 10:12], in0=cols[:, 0:2], scalar=0.0, in1=cols[:, 8:10],
                                           op0=ALU.max, op1=ALU.add).then_inc(sp_sum, 1)
            dve.wait_ge(ker_ln, 1)
            nc.vector.tensor_scalar(ker, ker, cols[:, 10:11], -1.0, ALU.mult, ALU.mult).then_inc(ker_ready, 1)
            dve.wait_ge(ker_ready, 1)
            nc.vector.scalar_tensor_tensor(out=ker_mask[:], in0=ker, scalar=cols[:, 2:3], in1=mask,
                                           op0=ALU.add, op1=ALU.add).then_inc(tables, 1)

            dve.wait_ge(pr_zeroed, 1)
            dve.wait_ge(angles, 32)

            for part in range(3):
                rope_queries(0, 0, part)
            for h in range(H):
                score_read(lambda j: (4 + j, j % 2), h, 0)
            qk_read(lambda j: (4 + H + j, j % 2), 1)

            def inverse_sums(b, ib, j):
                dve.wait_ge(exp_done, 64 * b + (16 * ib + 4 * j + 4))
                nc.vector.reciprocal(rsum[:, 4 * j:4 * j + 4], sums[:, 4 * j:4 * j + 4]).then_inc(rsum_ready, 1)

            def normalise(b, ib, j):
                dve.wait_ge(rsum_ready, 16 * b + (4 * ib + j) + 1)
                dve.sem_inc(norm_turn, 1)
                for t in range(4 * j, 4 * j + 4):
                    nc.vector.tensor_scalar(pr[:, t, keys(ib, t)], pr[:, t, keys(ib, t)], rsum[:, t:t + 1], None,
                                            ALU.mult).then_inc(norm_done, 1)

            def transposed(at, n_blocks, u):
                four, kb = divmod(u, n_blocks)
                k, bank = at
                dve.wait_ge(gap_fill, k + 1)
                nc.vector.tensor_copy(pT[:, kb, :, 4 * TQ * four:4 * TQ * (four + 1)],
                                      p_gap[:, bank, :].rearrange("p (i h) -> p h i", h=H)).then_inc(gap_read, 1)

            def values(at, G):
                k, bank = at
                dve.wait_ge(gap_fill, k + 1)
                nc.vector.tensor_copy(oT[:, :, GQ * G:GQ * G + GQ],
                                      p_gap[:, bank, :].rearrange("p (c n) -> p c n", n=GQ)).then_inc(gap_read, 1)

            def output(b, ib):
                n = 4 * b + (ib - 1)
                k, bank = unit(b, ib, "o")
                dve.wait_ge(y_stored, 16 * n + 16)
                dve.wait_ge(xf_loaded, 16 * n + 16)
                dve.wait_ge(gap_fill, k + 1)
                nc.vector.tensor_tensor(y[:], p_gap[:, bank, 0:D], xf[:], ALU.add).then_inc(gap_read, 1)

            def step(b, ib, last):
                more = not (last and ib == QB - 1)
                first = is_first(b, ib)

                def logits(t):
                    g = 64 * b + (16 * ib + t)
                    n_keys = TQ * (16 * ib + t + 1)
                    w = keys(ib, t)
                    dve.wait_ge(down_done, g + 1 + HIDS)
                    dve.wait_ge(sc_ready, g + 1 + RING)
                    dve.sem_inc(logit_turn, 1)
                    nc.vector.tensor_tensor_reduce(
                        out=pr[:, t, w], in0=p_down[:, t % 2, 0:n_keys], in1=pr[:, t, w],
                        scale=1.0, scalar=-3e38, op0=ALU.add, op1=ALU.max, accum_out=mx[:, t:t + 1])\
                        .then_inc(logit_done, 1)

                def negate_maxima(G):
                    r = slice(GT * G, GT * G + GT)
                    dve.wait_ge(logit_done, 64 * b + (16 * ib + GT * G + GT) + 2)
                    nc.vector.tensor_scalar(nmx[:, r], mx[:, r], -1.0, None, ALU.mult).then_inc(nmx_ready, 1)

                def value_read(j):
                    k, bank = unit(b, ib, "v", j)
                    dve.wait_ge(gap_fill, k + 1)
                    nc.vector.tensor_copy(vv[:, ib, j * L:(j + 1) * L], p_gap[:, bank, :]).then_inc(gap_read, 1)

                for r in range(GT):
                    if r >= LAG:
                        logits(r - LAG)
                    if not first:
                        for u in fillers_before(ib, r):
                            transposed(unit(b, ib, "t1", u), (ib - 1) % QB + 1, u)
                        if r == LAG - 1:
                            for j in (2, 3):
                                inverse_sums(*before(b, ib), j)
                            for j in (2, 3):
                                normalise(*before(b, ib), j)
                    for part, beside in enumerate(ROPE_BESIDE):
                        if r == beside and more:
                            rope_queries(*ahead(b, ib, 1), part)
                if not first:
                    values(unit(b, ib, "pv1"), 1)
                logits(GT - 2)
                logits(GT - 1)
                negate_maxima(0)
                value_read(0)
                if not first:
                    output(b, ib)
                value_read(1)
                for r in range(GT):
                    if r >= LAG:
                        logits(GT + r - LAG)
                    for kind, k in fillers(ib, r, more):
                        if kind == "scores":
                            score_read(lambda j: unit(b, ib, "scores", j), k, (ib + 1) % QB)
                        else:
                            transposed(unit(b, ib, "t0", k), ib + 1, k)
                    if r in (1, 2):
                        inverse_sums(b, ib, r - 1)
                        normalise(b, ib, r - 1)
                logits(TILES - 2)
                logits(TILES - 1)
                negate_maxima(1)
                values(unit(b, ib, "pv0"), 0)
                if not (last and ib >= QB - 2):
                    qk_read(lambda j: unit(b, ib, "qk", j), 4 * b + (ib + 2))

            over_batches(dve, step)
            for j in (2, 3):
                inverse_sums(B - 1, QB - 1, j)
                normalise(B - 1, QB - 1, j)
            for u in range(2 * QB):
                transposed(unit(B - 1, QB, "t1", u), QB, u)
            values(unit(B - 1, QB, "pv1"), 1)
            output(B - 1, QB)

        @block.tensor
        def _(pe):
            pe.sem_inc(up_done, RING)
            pe.sem_inc(down_done, HIDS)
            pe.wait_ge(wqkv_loaded, 16)

            def qk_unit(at, j, b, ib):
                k, bank = at(j)
                if j == 0:
                    pe.wait_ge(xT_loaded[ib], 16 * b + 16)
                pe.wait_ge(gap_read, k + 1)
                for i in range(4):
                    m = 4 * j + i
                    to, rows = p_gap[:, bank, i * P:(i + 1) * P], xT[:, ib, :]
                    if j < 2:
                        to, rows = to.rearrange("p (i t) -> p i t", i=TQ), by_query(rows)
                    last_mm = nc.tensor.matmul(to, wqkv[:, m * P:(m + 1) * P], rows, start=True, stop=True)
                last_mm.then_inc(gap_fill, 1)

            def scores_unit(at, h, b, ib):
                k, bank = at(h)
                if h == 0:
                    pe.wait_ge(ropeq, 4 * b + ib + 1)
                    pe.wait_ge(ropek, 4 * b + ib + 1)
                r = slice(HD * (h % 2), HD * (h % 2) + HD)
                n_keys = (ib + 1) * P
                pe.wait_ge(gap_read, k + 1)
                nc.tensor.matmul(p_gap[:, bank, 0:n_keys],
                                 raw[r, 0, h // 2, :], kk[r, h // 2, 0:n_keys], start=True, stop=True)\
                    .then_inc(gap_fill, 1)

            for j in range(4):
                qk_unit(lambda j: (j, j % 2), j, 0, 0)
            for h in range(H):
                scores_unit(lambda j: (4 + j, j % 2), h, 0, 0)
            for j in range(4):
                qk_unit(lambda j: (4 + H + j, j % 2), j, 0, 1)
            pe.wait_ge(consts, 16 * N_CONST)
            pe.wait_ge(ker_placed, 16 * 2 * RING)

            def transpose(at, b, ib, G, u):
                four, kb = divmod(u, ib + 1)
                k, bank = at
                if kb == 0:
                    pe.wait_ge(norm_done, 64 * b + (16 * ib + GT * G + 4 * four + 4))
                pe.wait_ge(gap_read, k + 1)
                c0 = L - (ib + 1 - kb) * P
                for i in range(4):
                    last_mm = nc.tensor.transpose(p_gap[:, bank, i * P:(i + 1) * P],
                                                  pr[:, GT * G + 4 * four + i, c0:c0 + P], ident[:])
                last_mm.then_inc(gap_fill, 1)

            def values(at, n_blocks):
                k, bank = at
                pe.wait_ge(gap_read, k + 2)
                for i in range(PAIRS):
                    for kb in range(n_blocks):
                        for r in range(2):
                            h = 2 * i + r
                            last_mm = nc.tensor.matmul(
                                p_gap[HD * r:HD * r + HD, bank, i * GQ:(i + 1) * GQ],
                                vv[:, kb, h * HD:(h + 1) * HD], pT[:, kb, h, :],
                                start=(kb == 0), stop=(kb == n_blocks - 1))
                last_mm.then_inc(gap_fill, 1)

            def output(b, ib):
                k, bank = unit(b, ib, "o")
                pe.wait_ge(gap_read, k + 2 - (ib < QB))
                for i in range(PAIRS):
                    last_mm = nc.tensor.matmul(p_gap[:, bank, 0:D], oT[:, i, :], wo[:, i, :],
                                               start=(i == 0), stop=(i == PAIRS - 1))
                last_mm.then_inc(gap_fill, 1)

            def step(b, ib, last):
                more = not (last and ib == QB - 1)
                first = is_first(b, ib)

                def up(t):
                    g = 64 * b + (16 * ib + t)
                    n_keys = TQ * (16 * ib + t + 1)
                    pe.wait_ge(x_loaded[t % RING], 32 * (64 // RING * b + (16 * ib + t) // RING) + 32)
                    pe.wait_ge(gelu_done, g + 1)
                    for half in range(2):
                        last_mm = nc.tensor.matmul(p_up[:, t % 2, half, 0:n_keys], w_up[:, half, :],
                                                   xa[:, half, t % RING, window(16 * ib + t)], start=True, stop=True)
                    last_mm.then_inc(up_done, 1)

                def down(t):
                    g = 64 * b + (16 * ib + t)
                    n_keys = TQ * (16 * ib + t + 1)
                    pe.wait_ge(logit_done, g + 1)
                    pe.wait_ge(gelu_done, g + 1 + 2)
                    for half in range(2):
                        last_mm = nc.tensor.matmul(p_down[HH * half:HH * half + HH, t % 2, 0:n_keys], w_down[:],
                                                   hid[:, t % HIDS, half, 0:n_keys], start=True, stop=True)
                    last_mm.then_inc(down_done, 1)

                def v_unit(j):
                    k, bank = unit(b, ib, "v", j)
                    pe.wait_ge(gap_read, k + 1)
                    v0 = 2 * H * HD + j * L
                    nc.tensor.matmul(p_gap[:, bank, :], xT[:, ib, :], wqkv[:, v0:v0 + L], start=True, stop=True)\
                        .then_inc(gap_fill, 1)

                for r in range(GT):
                    up(r)
                    if r >= LAG:
                        down(r - LAG)
                    if not first:
                        for u in fillers_before(ib, r):
                            transpose(unit(b, ib, "t1", u), *before(b, ib), 1, u)
                if not first:
                    values(unit(b, ib, "pv1"), (ib - 1) % QB + 1)
                down(GT - 2)
                down(GT - 1)
                v_unit(0)
                if not first:
                    output(b, ib)
                v_unit(1)
                for r in range(GT):
                    up(GT + r)
                    if r >= LAG:
                        down(GT + r - LAG)
                    for kind, k in fillers(ib, r, more):
                        if kind == "scores":
                            scores_unit(lambda j: unit(b, ib, "scores", j), k, *ahead(b, ib, 1))
                        else:
                            transpose(unit(b, ib, "t0", k), b, ib, 0, k)
                down(TILES - 2)
                down(TILES - 1)
                values(unit(b, ib, "pv0"), ib + 1)
                if not (last and ib >= QB - 2):
                    for j in range(4):
                        qk_unit(lambda j: unit(b, ib, "qk", j), j, *ahead(b, ib, 2))

            over_batches(pe, step)
            for u in range(2 * QB):
                transpose(unit(B - 1, QB, "t1", u), B - 1, QB - 1, 1, u)
            values(unit(B - 1, QB, "pv1"), QB)
            output(B - 1, QB)


def build(nc, a, c, out):
    xnT_dram = nc.dram_tensor("xnT_scratch", [CHUNKS, D, CH], F32, kind="Internal").ap()
    gT_dram = nc.dram_tensor("gT_scratch", [CHUNKS, P, CH], F32, kind="Internal").ap()
    xf_dram = nc.dram_tensor("xf_scratch", [ROWS, D], F32, kind="Internal").ap()
    x = a["L0_attn_x"].rearrange("b l d -> (b l) d")
    heads = lambda v: v.rearrange("h a b -> h (a b)")
    norm_and_gates(nc, x, a["L0_ffn_Wm"], a["L0_ffn_bm"], a["L0_ffn_expert_emb"], c, xnT_dram, gT_dram)
    experts(nc, x, a["L0_ffn_Wm"], a["L0_ffn_bm"], a["L0_ffn_W1"], a["L0_ffn_b1"], a["L0_ffn_W2"], a["L0_ffn_b2"],
            a["L0_ffn_Wo"], a["L0_ffn_bo"], c, xnT_dram, gT_dram, xf_dram)
    attention(nc, a["L0_attn_w_qkv"], a["L0_attn_w_o"], heads(a["L0_attn_log_p"]), heads(a["L0_attn_log_a"]),
              a["L0_attn_w1"], a["L0_attn_b1"], a["L0_attn_w2"], a["L0_attn_b2"], c, xnT_dram, xf_dram,
              out.rearrange("b l d -> (b l) d"))


_INS = ["L0_attn_x", "L0_attn_w_qkv", "L0_attn_w_o", "L0_attn_log_p", "L0_attn_log_a", "L0_attn_w1", "L0_attn_b1",
        "L0_attn_w2", "L0_attn_b2", "L0_ffn_Wm", "L0_ffn_bm", "L0_ffn_expert_emb", "L0_ffn_W1", "L0_ffn_b1",
        "L0_ffn_W2", "L0_ffn_b2", "L0_ffn_Wo", "L0_ffn_bo"]


def kernel(**inputs):
    import numpy as _np
    import concourse.bacc as _bacc
    from concourse import mybir as _mybir
    from concourse.bass_utils import run_bass_kernel_spmd as _run

    nc = _bacc.Bacc("TRN2", target_bir_lowering=False, num_devices=1)
    arrays, args, consts = {}, {}, {}
    for name in _INS:
        a = _np.ascontiguousarray(inputs[name])
        arrays[f"in_{name}"] = a
        args[name] = nc.dram_tensor(f"in_{name}", a.shape, _mybir.dt.from_np(a.dtype), kind="ExternalInput").ap()
    for name, a in shape_constants().items():
        a = _np.ascontiguousarray(a)
        arrays[name] = a
        consts[name] = nc.dram_tensor(name, a.shape, _mybir.dt.from_np(a.dtype), kind="ExternalInput").ap()
    out = nc.dram_tensor("out_0", (B, L, D), _mybir.dt.float32, kind="ExternalOutput").ap()
    build(nc, args, consts, out)
    r = _run(nc, [arrays], core_ids=[0])
    return r.results[0]["out_0"]
```
